# Optimizing a Trainium2 kernel written in Bass

```python
import numpy as np
import jax
import jax.numpy as jnp

def _softmax(x, axis=-1):
    return jax.nn.softmax(x, axis=axis)

def _gelu(x):
    return jax.nn.gelu(x, approximate=True)

def _silu(x):
    return jax.nn.silu(x)

def _sigmoid(x):
    return jax.nn.sigmoid(x)

def _layernorm(x, axis=-1, eps=1e-05):
    m = jnp.mean(x, axis=axis, keepdims=True)
    v = jnp.var(x, axis=axis, keepdims=True)
    return (x - m) / jnp.sqrt(v + eps)

def _scatter_add(tgt, idx, src, axis=0):
    return tgt.at[idx].add(src)

def _segment_sum(src, seg, n):
    return jax.ops.segment_sum(src, seg, n)
kernel_name = 'mk_macaron_d1_jaxref_r4_92d958'

def setup_inputs(seed: int=0):
    np.random.seed(seed)
    _w = jnp.asarray

    def _L0_attn_setup():
        import jax, jax.numpy as jnp
        import numpy as np
        D_MODEL = 512
        N_STATE = 64
        RANK = 64
        LEVELS = int(np.log2(N_STATE))
        B, S = (4, 1024)

        def _apply_butterfly(state, A_factors):
            b, s, n = state.shape
            x = state.reshape((b, s) + (2,) * LEVELS)
            for lvl in range(LEVELS):
                ax = 2 + lvl
                x = jnp.moveaxis(jnp.tensordot(x, A_factors[lvl], axes=[[ax], [0]]), -1, ax)
            return x.reshape(b, s, n)
        key = jax.random.key(seed)
        ks = jax.random.split(key, 7)
        u = jax.random.normal(ks[0], (B, S, D_MODEL), dtype=jnp.float32)
        A_factors = jax.random.normal(ks[1], (LEVELS, 2, 2), dtype=jnp.float32)
        A_factors = A_factors / jnp.linalg.norm(A_factors, axis=-1, keepdims=True)
        W_b_rank = jax.random.normal(ks[2], (D_MODEL, RANK), dtype=jnp.float32) * (1.0 / np.sqrt(D_MODEL))
        W_b_state = jax.random.normal(ks[3], (RANK, N_STATE), dtype=jnp.float32) * (1.0 / np.sqrt(RANK))
        W_c_rank = jax.random.normal(ks[4], (N_STATE, RANK), dtype=jnp.float32) * (1.0 / np.sqrt(N_STATE))
        W_c_model = jax.random.normal(ks[5], (RANK, D_MODEL), dtype=jnp.float32) * (1.0 / np.sqrt(RANK))
        D_vec = jax.random.normal(ks[6], (D_MODEL,), dtype=jnp.float32) * 0.02
        return {'u': u, 'A_factors': A_factors, 'W_b_rank': W_b_rank, 'W_b_state': W_b_state, 'W_c_rank': W_c_rank, 'W_c_model': W_c_model, 'D_vec': D_vec}
    _L0_attn_in = _L0_attn_setup()

    def _L0_ffn_setup():
        import jax, jax.numpy as jnp
        import numpy as np
        B, T, D = (2, 256, 512)
        H, K, DK = (4, 8, 64)
        E = 4096
        NK = 128
        key = jax.random.key(seed)
        k1, k2, k3, k4, k5 = jax.random.split(key, 5)
        x = jax.random.normal(k1, (B, T, D), dtype=jnp.float32)
        Wq = jax.random.normal(k2, (D, 2 * H * DK), dtype=jnp.float32) * 0.02
        keys = jax.random.normal(k3, (H, NK, 2, DK), dtype=jnp.float32) * 0.02
        e_down = jax.random.normal(k4, (E, D), dtype=jnp.float32) * 0.01
        e_up = jax.random.normal(k5, (E, D), dtype=jnp.float32) * 0.01
        return {'x': x, 'Wq': Wq, 'keys': keys, 'e_down': e_down, 'e_up': e_up}
    _L0_ffn_in = _L0_ffn_setup()
    _d = {'L0_attn_u': _L0_attn_in['u'], 'L0_attn_A_factors': _L0_attn_in['A_factors'], 'L0_attn_W_b_rank': _L0_attn_in['W_b_rank'], 'L0_attn_W_b_state': _L0_attn_in['W_b_state'], 'L0_attn_W_c_rank': _L0_attn_in['W_c_rank'], 'L0_attn_W_c_model': _L0_attn_in['W_c_model'], 'L0_attn_D_vec': _L0_attn_in['D_vec'], 'L0_ffn_Wq': _L0_ffn_in['Wq'], 'L0_ffn_keys': _L0_ffn_in['keys'], 'L0_ffn_e_down': _L0_ffn_in['e_down'], 'L0_ffn_e_up': _L0_ffn_in['e_up']}
    _x0 = _d['L0_attn_u']
    _d['L0_attn_u'] = jax.random.normal(jax.random.fold_in(jax.random.key(seed), 1), (8, 512, 512), dtype=_x0.dtype)
    del _x0
    return _d

def reference(L0_attn_u, L0_attn_A_factors, L0_attn_W_b_rank, L0_attn_W_b_state, L0_attn_W_c_rank, L0_attn_W_c_model, L0_attn_D_vec, L0_ffn_Wq, L0_ffn_keys, L0_ffn_e_down, L0_ffn_e_up):

    def _L0_attn_ref(u, A_factors, W_b_rank, W_b_state, W_c_rank, W_c_model, D_vec):
        import jax, jax.numpy as jnp
        import numpy as np
        D_MODEL = 512
        N_STATE = 64
        RANK = 64
        LEVELS = int(np.log2(N_STATE))
        B, S = (4, 1024)

        def _apply_butterfly(state, A_factors):
            b, s, n = state.shape
            x = state.reshape((b, s) + (2,) * LEVELS)
            for lvl in range(LEVELS):
                ax = 2 + lvl
                x = jnp.moveaxis(jnp.tensordot(x, A_factors[lvl], axes=[[ax], [0]]), -1, ax)
            return x.reshape(b, s, n)
        state = u @ W_b_rank @ W_b_state
        state = _apply_butterfly(state, A_factors)
        y = state @ W_c_rank @ W_c_model
        return y + D_vec * u

    def _L0_ffn_ref(x, Wq, keys, e_down, e_up):
        import jax, jax.numpy as jnp
        import numpy as np
        B, T, D = (2, 256, 512)
        H, K, DK = (4, 8, 64)
        E = 4096
        NK = 128
        b, t, d = x.shape
        q = (x @ Wq).reshape(b, t, H, 2, DK)
        q1, q2 = (q[..., 0, :], q[..., 1, :])
        sim1 = jnp.einsum('bthd,hkd->bthk', q1, keys[:, :, 0, :])
        sim2 = jnp.einsum('bthd,hkd->bthk', q2, keys[:, :, 1, :])
        s1, i1 = jax.lax.top_k(sim1, K)
        s2, i2 = jax.lax.top_k(sim2, K)
        all_scores = (s1[..., :, None] + s2[..., None, :]).reshape(b, t, H, K * K)
        all_indices = (i1[..., :, None] * NK + i2[..., None, :]).reshape(b, t, H, K * K)
        final_scores, pk_idx = jax.lax.top_k(all_scores, K)
        final_indices = jnp.take_along_axis(all_indices, pk_idx, axis=-1)
        w_down = e_down[final_indices]
        w_up = e_up[final_indices]
        hidden = jnp.einsum('btd,bthkd->bthk', x, w_down)
        hidden = jax.nn.silu(hidden)
        hidden = hidden * jax.nn.relu(final_scores)
        out = jnp.einsum('bthk,bthkd->btd', hidden, w_up)
        return out
    x = L0_attn_u
    x = x + 0.5 * _L0_ffn_ref(_layernorm(x, axis=-1), L0_ffn_Wq, L0_ffn_keys, L0_ffn_e_down, L0_ffn_e_up)
    x = x + _L0_attn_ref(_layernorm(x, axis=-1), L0_attn_A_factors, L0_attn_W_b_rank, L0_attn_W_b_state, L0_attn_W_c_rank, L0_attn_W_c_model, L0_attn_D_vec)
    x = x + 0.5 * _L0_ffn_ref(_layernorm(x, axis=-1), L0_ffn_Wq, L0_ffn_keys, L0_ffn_e_down, L0_ffn_e_up)
    return x

_drawn_inputs = setup_inputs


def setup_inputs(seed=0):
    import zlib

    import numpy as np

    out = dict(_drawn_inputs(seed))
    spreads = {}
    factors = {'L0_attn_D_vec': 14.709,
     'L0_ffn_Wq': 8.0,
     'L0_ffn_keys': 8.0,
     'L0_ffn_e_down': 8.0,
     'L0_ffn_e_up': 8.0}
    for name, (base, spread) in spreads.items():
        noise = np.random.default_rng([zlib.crc32(name.encode()), seed]).standard_normal(out[name].shape)
        drawn = base * np.exp(spread * noise) if base else spread * noise
        out[name] = jnp.asarray(drawn.astype(out[name].dtype))
    for name, factor in factors.items():
        out[name] = (out[name] * factor).astype(out[name].dtype)
    return out
```

```python
from contextlib import ExitStack

import concourse.bass as bass
from concourse import mybir

F32 = mybir.dt.float32
F32R = mybir.dt.float32r
BF16 = mybir.dt.bfloat16
U32 = mybir.dt.uint32
ALU = mybir.AluOpType
ACT = mybir.ActivationFunctionType
AX = mybir.AxisListType
ds = bass.ds

P = 128
H, L = 0, 1


def macaron(nc, u, A_factors, W_b_rank, W_b_state, W_c_rank, W_c_model, D_vec, Wq, keys, e_down, e_up, y_all):
    D = u.shape[2]
    NTOK = u.shape[0] * u.shape[1]
    BLK = 512
    NT = BLK // P
    NBLK = NTOK // BLK
    KC = D // P
    HEADS, NK, _, DK = keys.shape
    TOP = 8
    HK = HEADS * TOP
    E = e_down.shape[0]
    STEPS = E // P
    HALF = STEPS // 2
    RANK = W_b_rank.shape[1]
    LEVELS = A_factors.shape[0]
    EPS = 1e-5
    NG = 32
    TG = P // NG
    GB = 8
    NB = NG // GB
    PER = 4
    ITERS = STEPS // PER
    NSTAGE = 2 * NBLK
    LAG = 2
    assert NK == P and HK == 32 and 2 * DK == P and TG * HK == P and NB == PER and BLK == 512 and D == 512

    u_t = u.rearrange("b (t p) d -> b t p d", p=P)
    x_in = nc.dram_tensor("x_in", (NSTAGE + 2, NT, P, D), F32, kind="Internal").ap()
    wd_dram = nc.dram_tensor("wd_split", (STEPS, P, 2 * D), F32, kind="Internal").ap()
    wu_dram = nc.dram_tensor("wu_split", (STEPS, P, 2 * D), F32, kind="Internal").ap()
    ed_t = e_down.rearrange("(s p) d -> s p d", p=P)
    eu_t = e_up.rearrange("(s p) d -> s p d", p=P)

    with ExitStack() as ctx:
        def sb(name, shape, dt=F32):
            return ctx.enter_context(nc.sbuf_tensor(name, shape, dt))

        def sem(name):
            return ctx.enter_context(nc.semaphore(name))

        G = sb("G", [P, STEPS, BLK])
        wd = sb("wd", [P, 2, 2 * D], F32R)
        wu = sb("wu", [P, 2, 2 * D], F32R)
        xT = sb("xT", [P, 2, 2, KC, BLK], F32R)
        act = sb("act", [P, 2, BLK])
        hid = sb("hid", [P, PER, 2, BLK], F32R)
        wq = sb("wq", [P, 2, KC, HEADS * P], F32R)
        kb = sb("kb", [P, 2, HEADS, 2 * NK], F32R)
        pick = sb("pick", [P, 2, NT, 5, NG])
        hot1 = sb("hot1", [P, 2, 3, GB, TG * HALF], BF16)
        hot1_eq = sb("hot1_eq", [P, GB, TG * HALF], BF16)
        hot2 = sb("hot2", [P, 2, GB, P], BF16)
        xs = sb("xs", [P, D])
        xln = sb("xln", [P, D])
        qT = sb("qT", [P, 2, HEADS * P], F32R)
        sims = sb("sims", [P, 2, 2, NK])
        yres = sb("yres", [P, NT, D])
        xa = sb("xa", [P, D])
        xaln = sb("xaln", [P, D])
        xaT = sb("xaT", [P, KC, P])
        zT = sb("zT", [RANK, P])
        M = sb("M", [RANK, D])
        wb = sb("wb", [P, KC, RANK])
        Dv = sb("Dv", [P, D])
        v8 = sb("v8", [P, HEADS, 2, TOP])
        i8 = sb("i8", [P, HEADS, 2, TOP], U32)
        s64 = sb("s64", [P, HEADS, TOP, TOP])
        f8 = sb("f8", [P, HEADS, TOP])
        pos = sb("pos", [P, HK], U32)
        j12 = sb("j12", [P, 2, HK], U32)
        eq8 = sb("eq8", [P, 2, HK, TOP], BF16)
        i12 = sb("i12", [P, 2, HK])
        clamp = sb("clamp", [P, HK])
        raw = sb("raw", [P, 3, HK])
        rest = sb("rest", [P, 2, HK])
        part = sb("part", [P, 2, HK], BF16)
        stat = sb("stat", [P, 12])
        stata = sb("stata", [P, 12])
        iota1 = sb("iota1", [P, 2, TG * HALF], BF16)
        iota2 = sb("iota2", [P, P], BF16)
        iota8 = sb("iota8", [P, TOP], BF16)
        tq = sb("tq", [P, 1])
        nhalf = sb("nhalf", [P, 1])
        ident = sb("ident", [P, P])
        zer = sb("zer", [P, D], BF16)
        ones = s64[0:1, 0:2, :, :].rearrange("p a b c -> p (a b c)")

        ps_out = [ctx.enter_context(nc.psum_tensor(f"ps_out{t}", [P, D], F32)) for t in range(NT)]
        ps_hd = [ctx.enter_context(nc.psum_tensor(f"ps_hd{t}", [P, BLK], F32)) for t in range(2)]
        ps_s = ctx.enter_context(nc.psum_tensor("ps_s", [P, 512], F32))
        ps_g = ctx.enter_context(nc.psum_tensor("ps_g", [P, GB, TG, HALF], F32))

        consts = sem("consts")
        tq_set = sem("tq_set")
        const_c = sem("const_c")
        small_in = sem("small_in")
        fac_in = sem("fac_in")
        x_copied = sem("x_copied")
        raw_in = [sem(f"raw_in{j}") for j in range(PER)]
        w_tr = sem("w_tr")
        w_h = sem("w_h")
        w_l = sem("w_l")
        w_uh = sem("w_uh")
        w_ul = sem("w_ul")
        w_out = [sem(f"w_out{j}") for j in range(2)]
        k_tr = sem("k_tr")
        k_h = sem("k_h")
        k_l = sem("k_l")
        fly = sem("fly")
        a_pe = sem("a_pe")
        a_cp = sem("a_cp")
        wd_in = [sem(f"wd_in{j}") for j in range(2)]
        wu_in = [sem(f"wu_in{j}") for j in range(2)]
        down_done = sem("down_done")
        silu_done = sem("silu_done")
        mult_done = sem("mult_done")
        hidh_done = sem("hidh_done")
        hidl_done = sem("hidl_done")
        up_done = sem("up_done")
        evac_done = sem("evac_done")
        res_in = sem("res_in")
        block_out = sem("block_out")
        hot2_done = sem("hot2_done")
        hot1_eqd = sem("hot1_eqd")
        hot1_done = sem("hot1_done")
        g_mm = sem("g_mm")
        g_out = sem("g_out")
        x_in_s = sem("x_in_s")
        sel_c = sem("sel_c")
        rstd_done = sem("rstd_done")
        s_t = sem("s_t")
        s_xh = sem("s_xh")
        s_xl = sem("s_xl")
        s_q = sem("s_q")
        s_qh = sem("s_qh")
        s_ql = sem("s_ql")
        s_sim = sem("s_sim")
        s_simc = sem("s_simc")
        split_c = sem("split_c")
        picked = sem("picked")
        xa_in = sem("xa_in")
        att_c = sem("att_c")
        arstd_done = sem("arstd_done")
        a_t = sem("a_t")
        a_x = sem("a_x")
        a_z = sem("a_z")
        a_zc = sem("a_zc")
        a_y = sem("a_y")
        a_du = sem("a_du")
        a_fin = sem("a_fin")
        a_out = sem("a_out")
        apart = {n: sem(f"apart_{n}") for n in ("sp", "act", "dve", "pool", "pe")}
        block = ctx.enter_context(nc.Block())

        def held(eng, name, s, value):
            if isinstance(value, int):
                if value > 0:
                    eng.wait_ge(s, value)
                return
            eng.wait_ge(s, value)
            eng.sem_inc(apart[name], 1)

        def stages(eng, body):
            for n0, n1, attn in ((0, LAG, False), (LAG, NBLK + LAG, True), (NBLK + LAG, NSTAGE, False)):
                with eng.Fori(0, (n1 - n0) // 2) as m:
                    with eng.Fori(0, 2) as p:
                        body(eng.snap(m * 2 + p + n0), p, attn)

        def iterations(eng, n, p, attn, run_a, run_b, between=None):
            with eng.Fori(1, NT) as t:
                run_a(eng.snap(n * ITERS + t), n, p, t)
            if between:
                between(n)
            with eng.Fori(0, NT) as t:
                run_b(eng.snap(n * ITERS + NT + t), n, p, t, attn)
            run_a(eng.snap(n * ITERS + ITERS), n + 1, 1 - p, 0)

        SEL_IDX0, SEL_IDX1, SEL = 12, 20, 33
        ATT = 4


        @block.sync
        def _(sp):
            sp.dma_start(G[:, 0:KC, :], Wq.rearrange("(c p) n -> p c n", p=P)).then_inc(small_in, 16)
            sp.dma_start(G[:, KC, :], keys.rearrange("h k s d -> k h (s d)")).then_inc(small_in, 16)
            sp.dma_start(wb[:], W_b_rank.rearrange("(c p) r -> p c r", p=P)).then_inc(small_in, 16)
            sp.dma_start(xaT[0:RANK, 0, 0:RANK], W_b_state).then_inc(small_in, 16)
            sp.dma_start(xaT[0:RANK, 1, 0:RANK], W_c_rank).then_inc(small_in, 16)
            sp.dma_start(xaln[0:RANK, :], W_c_model).then_inc(small_in, 16)
            sp.dma_start(xa[0:1, 0:LEVELS * 4], A_factors.rearrange("(o l) a b -> o (l a b)", o=1)).then_inc(small_in, 16)
            sp.dma_start(xs[0:1, :], D_vec.rearrange("(o d) -> o d", o=1)).then_inc(a_out, 16)

            def raw_load(i, j):
                held(sp, "sp", w_l, (i - 1) * PER + j + 1 if not isinstance(i, int) else 0)
                held(sp, "sp", w_ul, (i - 1) * PER + j + 1 if not isinstance(i, int) else 0)
                sp.dma_start(G[:, 8 + j, :], ed_t[i * PER + j]).then_inc(raw_in[j], 16)
                sp.dma_start(G[:, 12 + j, :], eu_t[i * PER + j]).then_inc(raw_in[j], 16)

            for j in range(PER):
                raw_load(0, j)
            with sp.Fori(1, STEPS // PER) as i:
                for j in range(PER):
                    raw_load(i, j)

            sp.wait_ge(x_copied, 16)
            for q in range(NT):
                held(sp, "sp", s_t, q)
                sp.dma_start(xs[:], x_in[0, q]).then_inc(x_in_s, 16)
            for j in range(2):
                sp.wait_ge(w_out[j], 16 * STEPS)

            def load_down(it, j, step):
                held(sp, "sp", down_done, it * PER + j - 1 if not isinstance(it, int) else max(0, it * PER + j - 1))
                sp.dma_start(wd[:, j % 2, :].bitcast(F32), wd_dram[step]).then_inc(wd_in[j % 2], 16)

            def load_up(it, j, step):
                held(sp, "sp", up_done, (it - 1) * PER + j - 1)
                sp.dma_start(wu[:, j % 2, :].bitcast(F32), wu_dram[step]).then_inc(wu_in[j % 2], 16)

            load_down(0, 0, 0)
            load_down(0, 1, 1)
            for j in range(2):
                sp.dma_start(wu[:, j, :].bitcast(F32), wu_dram[j]).then_inc(wu_in[j], 16)
            for t in range(2):
                sp.wait_ge(s_t, NT + t)
                sp.dma_start(xs[:], x_in[1, t]).then_inc(x_in_s, 16)
            load_down(0, 2, 2)
            load_down(0, 3, 3)

            def stream(it, up0, down0, next_up):
                for j in range(PER):
                    if j < 2:
                        load_down(it, j, down0 + j)
                        load_up(it, j + 2, up0 + j + 2)
                    else:
                        load_down(it, j, down0 + j)
                        load_up(it + 1, j - 2, next_up + j - 2)

            def run_a(it, n, p, t):
                if isinstance(t, int):
                    stream(it, STEPS - PER, 0, 0)
                    held(sp, "sp", s_t, n * NT + NT + 1)
                    sp.dma_start(xs[:], x_in[n + 1, 1]).then_inc(x_in_s, 16)
                else:
                    stream(it, t * PER - PER, t * PER, t * PER)
                    held(sp, "sp", s_t, n * NT + NT + t + 1)
                    with_next = sp.snap(n * NT + NT + t + 1)
                    sp.dma_start(xs[:], x_in.rearrange("s t p d -> (s t) p d")[with_next]).then_inc(x_in_s, 16)

            def run_b(it, n, p, t, attn):
                if attn:
                    r = (n - LAG) * NT + t
                    held(sp, "sp", a_fin, r + 1)
                    sp.dma_start(xa[:], y_all.rearrange("s t p d -> (s t) p d")[sp.snap((n - LAG) * NT + t)]).then_inc(xa_in, 16)
                stream(it, HALF - PER + t * PER, HALF + t * PER, HALF + t * PER)

            def residual(n):
                held(sp, "sp", block_out, n * 16 + 16)
                sp.dma_start(yres[:], x_in[n].rearrange("t p d -> p t d")).then_inc(res_in, 16)

            for n0, n1, attn in ((0, LAG, False), (LAG, NBLK + LAG, True), (NBLK + LAG, NSTAGE, False)):
                if n0 == NBLK + LAG:
                    sp.wait_ge(a_out, 16 + 16 * NT * NBLK)
                with sp.Fori(0, (n1 - n0) // 2) as m:
                    with sp.Fori(0, 2) as p:
                        n = sp.snap(m * 2 + p + n0)
                        if attn:
                            held(sp, "sp", a_out, n * (16 * NT) - (LAG * 16 * NT - 16))
                        iterations(sp, n, p, attn, run_a, run_b, residual)
            sp.wait_ge(block_out, 16 * (NSTAGE + 1))
            for j in range(2):
                sp.wait_ge(wd_in[j], 16 * (STEPS * NSTAGE // 2 + 2))
                sp.wait_ge(wu_in[j], 16 * (STEPS * NSTAGE // 2 + 1))
            sp.wait_ge(x_in_s, 16 * (NT * (NSTAGE + 1) + 2))

        @block.gpsimd
        def _(pool):
            def mark(ins):
                ins.then_inc(const_c, 1)

            mark(pool.memset(ident[:], 0.0))
            mark(pool.memset(zer[:], 0.0))
            mark(pool.memset(ones, 1.0))
            mark(pool.memset(nhalf[:], -0.5))
            for h in range(2):
                mark(pool.iota(iota1[:, h, :], pattern=[[HK, TG], [1, HALF]], base=HALF * h, channel_multiplier=0,
                               allow_small_or_imprecise_dtypes=True))
            mark(pool.iota(iota2[:], pattern=[[1, P]], base=0, channel_multiplier=0, allow_small_or_imprecise_dtypes=True))
            mark(pool.iota(iota8[:], pattern=[[1, TOP]], base=0, channel_multiplier=0, allow_small_or_imprecise_dtypes=True))
            mark(pool.memset(kb[:].bitcast(F32), 0.0))
            pool.wait_ge(const_c, 9)
            pool.affine_select(out=ident[:], in_=ident[:], compare_op=ALU.not_equal, fill=1.0, base=0,
                               pattern=[[-1, P]], channel_multiplier=1).then_inc(consts, 1)

            def split_up(i, j):
                held(pool, "pool", raw_in[j], i * 32 + 32)
                held(pool, "pool", w_out[j % 2], i * (PER // 2 * 32) + (j // 2) * 32)
                pool.tensor_copy(wu[:, j % 2, 0:D], G[:, 12 + j, :]).then_inc(w_uh, 1)
                held(pool, "pool", w_uh, i * PER + j + 1)
                pool.tensor_tensor(wu[:, j % 2, D:2 * D], G[:, 12 + j, :], wu[:, j % 2, 0:D].bitcast(F32),
                                   ALU.subtract).then_inc(w_ul, 1)

            for j in range(PER):
                split_up(0, j)
            with pool.Fori(1, STEPS // PER) as i:
                for j in range(PER):
                    split_up(i, j)

            def rstd(q):
                held(pool, "pool", sel_c, q * SEL + 3)
                pool.tensor_tensor(stat[:, 8:9], stat[:, 7:8], nhalf[:], ALU.pow).then_inc(rstd_done, 1)

            def arstd(r):
                held(pool, "pool", att_c, r * ATT + 3)
                pool.tensor_tensor(stata[:, 8:9], stata[:, 7:8], nhalf[:], ALU.pow).then_inc(arstd_done, 1)

            def hot1_scores(gb, b, par, t):
                held(pool, "pool", g_mm, gb - 1 if not isinstance(gb, int) else max(0, gb - 1))
                held(pool, "pool", hot1_eqd, gb + 1)
                for k in range(3):
                    ins = pool.tensor_tensor(hot1[:, b % 2, k, :, :], hot1_eq[:],
                                             pick[:, par, t, 2 + k, b * GB:b * GB + GB].unsqueeze(2).to_broadcast(
                                                 [P, GB, TG * HALF]), ALU.mult)
                ins.then_inc(hot1_done, 1)

            def hid_low(S, j):
                held(pool, "pool", hidh_done, S + 1)
                pool.tensor_tensor(hid[:, j, L, :], act[:, j % 2, :], hid[:, j, H, :].bitcast(F32),
                                   ALU.subtract).then_inc(hidl_done, 1)

            for q in range(NT):
                rstd(q)
            pool.wait_ge(picked, NT)
            for t in range(NT):
                for b in range(NB):
                    hot1_scores(t * NB + b, b, 0, t)

            def run_a(it, n, p, t):
                first = isinstance(it, int)
                rstd(n * NT + NT + t)
                for b in range(NB):
                    hot1_scores(it * NB + NT * NB + b, b, p, t)
                    if b or not first:
                        hid_low(it * PER + b - 1, (b - 1) % PER)

            def run_b(it, n, p, t, attn):
                if attn:
                    r = pool.snap((n - LAG) * NT + t)
                    arstd(r)
                held(pool, "pool", picked, n * NT + NT + t + 1)
                for b in range(NB):
                    hot1_scores(it * NB + NT * NB + b, b, 1 - p, t)
                    hid_low(it * PER + b - 1, (b - 1) % PER)
                    if attn and b == 1:
                        held(pool, "pool", a_t, r + 1)
                        pool.tensor_tensor(xaln[:], xaln[:], Dv[:], ALU.mult).then_inc(a_du, 1)
                        held(pool, "pool", a_du, r * 2 + 1)
                        pool.tensor_tensor(xaln[:], xaln[:], xa[:], ALU.add).then_inc(a_du, 1)

            run_a(0, 0, 0, 0)
            stages(pool, lambda n, p, attn: iterations(pool, n, p, attn, run_a, run_b))

        @block.scalar
        def _(sc):
            sc.preload_act_table(ACT.Silu)
            sc.dma_start(x_in[0:NBLK], u_t).then_inc(x_copied, 16)
            sc.dma_start(x_in[NSTAGE:NSTAGE + 2], u_t[0:2]).then_inc(block_out, 16)

            def split_down(i, j):
                held(sc, "act", w_tr, i * PER + j + 1)
                held(sc, "act", w_out[j % 2], i * (PER // 2 * 32) + (j // 2) * 32)
                sc.copy(wd[:, j % 2, 0:D], ps_hd[j % 2][:]).then_inc(w_h, 1)
                held(sc, "act", w_l, i * PER + j + 1)
                sc.dma_start(wd_dram[i * PER + j], wd[:, j % 2, :].bitcast(F32)).then_inc(w_out[j % 2], 16)
                held(sc, "act", w_ul, i * PER + j + 1)
                sc.dma_start(wu_dram[i * PER + j], wu[:, j % 2, :].bitcast(F32)).then_inc(w_out[j % 2], 16)

            sc.wait_ge(small_in, 16 * 7)
            sc.copy(wq[:, H, :, :], G[:, 0:KC, :]).then_inc(k_h, 1)
            sc.wait_ge(k_tr, 1)
            for s in range(2):
                rows = slice(DK * s, DK * s + DK)
                sc.copy(kb[rows, H, :, s * NK:s * NK + NK],
                        ps_s[rows, :].rearrange("p (h k) -> p h k", h=HEADS)).then_inc(k_h, 1)
            for j in range(PER):
                split_down(0, j)
            with sc.Fori(1, STEPS // PER) as i:
                for j in range(PER):
                    split_down(i, j)

            def x_high(q, par, t):
                held(sc, "act", s_t, q + 1)
                sc.copy(xT[:, par, H, :, ds(t * P, P)], ps_s[:].rearrange("p (c n) -> p c n", c=KC)).then_inc(s_xh, 1)

            def q_high(q):
                sc.wait_ge(s_q, q + 1)
                sc.copy(qT[:, H, :], ps_s[:]).then_inc(s_qh, 1)

            def sim_copy(q, h2):
                free = q * SEL + (SEL_IDX0 if h2 else SEL_IDX1 - SEL)
                held(sc, "act", sel_c, max(0, free) if isinstance(free, int) else free)
                held(sc, "act", s_sim, q * 2 + h2 + 1)
                sc.copy(sims[:].rearrange("p a b c -> p (a b c)"), ps_s[:]).then_inc(s_simc, 1)

            def g_evac(gb, b, half, t):
                held(sc, "act", g_mm, gb + 1)
                view = G[:, half * HALF:half * HALF + HALF, :].rearrange("p i (a q g) -> p i a q g", a=NT, q=TG)
                sc.copy(view[:, :, t, :, b * GB:b * GB + GB].rearrange("p i q g -> p g q i"), ps_g[:]).then_inc(g_out, 1)

            def silu(S, j):
                held(sc, "act", hidl_done, S - 1 if not isinstance(S, int) else max(0, S - 1))
                held(sc, "act", down_done, S + 1)
                sc.activation(act[:, j % 2, :], ps_hd[j % 2][:], ACT.Silu).then_inc(silu_done, 1)

            def hid_high(S, j):
                sc.wait_ge(mult_done, S + 1)
                sc.copy(hid[:, j, H, :], act[:, j % 2, :]).then_inc(hidh_done, 1)

            def select_whole(q, par, t):
                x_high(q, par, t)
                q_high(q)
                sim_copy(q, 0)
                sim_copy(q, 1)

            for q in range(NT):
                select_whole(q, 0, q)
            for t in range(NT):
                for b in range(NB):
                    g_evac(t * NB + b, b, 0, t)

            def run_a(it, n, p, t):
                first = isinstance(it, int)
                q = 4 if first else sc.snap(n * NT + NT + t)
                q_par = 1 if first else 1 - p
                held(sc, "act", mult_done, it * PER)
                for b in range(NB):
                    if b == 0:
                        x_high(q, q_par, t)
                    if b == 1:
                        sim_copy(q, 0)
                    if b == 2:
                        sim_copy(q, 1)
                    silu(it * PER + b, b)
                    if b or not first:
                        hid_high(it * PER + b - 1, (b - 1) % PER)
                    g_evac(it * NB + NT * NB + b, b, 1, t)
                    if b == 0:
                        q_high(q)

            def run_b(it, n, p, t, attn):
                r = sc.snap((n - LAG) * NT + t) if attn else None
                held(sc, "act", mult_done, it * PER)
                for b in range(NB):
                    if attn and b == 1:
                        sc.wait_ge(a_t, r + 1)
                        sc.copy(xaT[:].rearrange("p c n -> p (c n)"), ps_s[:]).then_inc(a_x, 1)
                    if attn and b == 2:
                        sc.wait_ge(a_z, r + 1)
                        sc.copy(zT[:], ps_s[0:RANK, 0:P]).then_inc(a_zc, 1)
                    silu(it * PER + b, b)
                    hid_high(it * PER + b - 1, (b - 1) % PER)
                    g_evac(it * NB + NT * NB + b, b, 0, t)
                    if attn and b == 3:
                        held(sc, "act", a_fin, r + 2)
                        sc.dma_start(x_in.rearrange("s t p d -> (s t) p d")[sc.snap((n - LAG + NBLK) * NT + t)],
                                     xaln[:]).then_inc(a_out, 16)

            run_a(0, 0, 0, 0)

            def body(n, p, attn):
                iterations(sc, n, p, attn, run_a, run_b)
                held(sc, "act", evac_done, n * NT + NT)
                sc.dma_start(y_all[n].rearrange("t p d -> p t d"), yres[:]).then_inc(block_out, 16)

            stages(sc, body)
            sc.wait_ge(a_out, 16 + 16 * NT * NBLK)
            sc.wait_ge(x_copied, 16)

        @block.vector
        def _(dve):
            for t in range(TG):
                dve.memset(tq[NG * t:NG * t + NG, :], float(HK * t)).then_inc(tq_set, 1)
            dve.wait_ge(tq_set, TG)
            dve.wait_ge(consts, 1)
            dve.wait_ge(small_in, 16 * 7)
            dve.wait_ge(k_h, 1)
            dve.tensor_tensor(wq[:, L, :, :], G[:, 0:KC, :], wq[:, H, :, :].bitcast(F32), ALU.subtract).then_inc(k_l, 1)
            dve.wait_ge(k_h, 3)
            for s in range(2):
                rows = slice(DK * s, DK * s + DK)
                dve.tensor_tensor(kb[rows, L, :, s * NK:s * NK + NK], ps_s[rows, :].rearrange("p (h k) -> p h k", h=HEADS),
                                  kb[rows, H, :, s * NK:s * NK + NK].bitcast(F32), ALU.subtract).then_inc(k_l, 1)
            dve.wait_ge(a_pe, 1)
            dve.tensor_copy(stata[0:RANK, 0:12], ps_s[0:RANK, 0:12]).then_inc(fly, 1)
            dve.tensor_copy(stat[0:RANK, 0:12], ps_s[0:RANK, 12:24]).then_inc(fly, 1)
            c = 2

            def factor(lvl, i, j):
                at = lvl * 4 + i * 2 + j
                return stata[0:RANK, at:at + 1] if at < 12 else stat[0:RANK, at - 12:at - 11]

            for lvl in range(LEVELS):
                src = xaT[0:RANK, 0 if lvl % 2 == 0 else 2, 0:RANK].rearrange("r (a i b) -> r a i b", a=2 ** lvl, i=2)
                dst = xaT[0:RANK, 2 if lvl % 2 == 0 else 0, 0:RANK].rearrange("r (a i b) -> r a i b", a=2 ** lvl, i=2)
                dve.wait_ge(fly, c)
                for j in range(2):
                    dve.tensor_scalar(dst[:, :, j, :], src[:, :, 0, :], factor(lvl, 0, j), None, ALU.mult).then_inc(fly, 1)
                c += 2
                dve.wait_ge(fly, c)
                for j in range(2):
                    dve.scalar_tensor_tensor(out=dst[:, :, j, :], in0=src[:, :, 1, :], scalar=factor(lvl, 1, j),
                                             in1=dst[:, :, j, :], op0=ALU.mult, op1=ALU.add).then_inc(fly, 1)
                c += 2
            dve.wait_ge(a_pe, 2)
            dve.tensor_copy(Dv[:], ps_g[:].rearrange("p g q i -> p (g q i)")).then_inc(a_cp, 1)
            dve.wait_ge(a_pe, 3)
            dve.tensor_copy(xaT[0:RANK, 3, 0:RANK], ps_s[0:RANK, 0:RANK]).then_inc(a_cp, 1)
            dve.wait_ge(a_pe, 4)
            dve.tensor_copy(xaT[0:RANK, 2, 0:RANK], ps_s[0:RANK, 0:RANK]).then_inc(a_cp, 1)
            dve.wait_ge(a_pe, 5)
            dve.tensor_copy(M[:], ps_s[0:RANK, :]).then_inc(a_fin, 1)

            def low_down(i, j):
                held(dve, "dve", w_h, i * PER + j + 1)
                dve.tensor_tensor(wd[:, j % 2, D:2 * D], ps_hd[j % 2][:], wd[:, j % 2, 0:D].bitcast(F32),
                                  ALU.subtract).then_inc(w_l, 1)

            for j in range(PER):
                low_down(0, j)
            with dve.Fori(1, STEPS // PER) as i:
                for j in range(PER):
                    low_down(i, j)

            def normalise(x, out, st, chain, base, done, number):
                dve.bn_stats(st[:, 0:6], x[:]).then_inc(chain, 1)
                held(dve, "dve", chain, base + 1)
                dve.bn_aggr(st[:, 6:8], st[:, 0:6]).then_inc(chain, 1)
                held(dve, "dve", chain, base + 2)
                dve.tensor_scalar(st[:, 7:8], st[:, 7:8], EPS, None, ALU.add).then_inc(chain, 1)
                held(dve, "dve", done, number + 1)
                dve.tensor_scalar(out[:], x[:], st[:, 6:7], st[:, 8:9], ALU.subtract, ALU.mult).then_inc(chain, 1)

            def sel_norm(q):
                held(dve, "dve", x_in_s, q * 16 + 16)
                held(dve, "dve", s_t, q)
                normalise(xs, xln, stat, sel_c, q * SEL, rstd_done, q)

            def x_low(q, par, t):
                held(dve, "dve", s_xh, q + 1)
                dve.tensor_tensor(xT[:, par, L, :, ds(t * P, P)], ps_s[:].rearrange("p (c n) -> p c n", c=KC),
                                  xT[:, par, H, :, ds(t * P, P)].bitcast(F32), ALU.subtract).then_inc(s_xl, 1)

            def q_low(q):
                held(dve, "dve", s_qh, q + 1)
                dve.tensor_tensor(qT[:, L, :], ps_s[:], qT[:, H, :].bitcast(F32), ALU.subtract).then_inc(s_ql, 1)

            def best(q, h2):
                held(dve, "dve", s_simc, q * 2 + h2 + 1)
                for h in range(2):
                    for s in range(2):
                        dve.max(v8[:, 2 * h2 + h, s, :], sims[:, h, s, :]).then_inc(sel_c, 1)
                held(dve, "dve", sel_c, q * SEL + 8 * (h2 + 1))
                for h in range(2):
                    for s in range(2):
                        dve.max_index(i8[:, 2 * h2 + h, s, :], v8[:, 2 * h2 + h, s, :], sims[:, h, s, :]).then_inc(sel_c, 1)

            def merge(q, par, t):
                base = q * SEL

                def after(k):
                    held(dve, "dve", sel_c, base + k)

                after(20)
                dve.tensor_tensor(s64[:], v8[:, :, 0, :].unsqueeze(3).to_broadcast([P, HEADS, TOP, TOP]),
                                  v8[:, :, 1, :].unsqueeze(2).to_broadcast([P, HEADS, TOP, TOP]), ALU.add).then_inc(sel_c, 1)
                after(21)
                for h in range(HEADS):
                    ins = dve.max(f8[:, h, :], s64[:, h, :, :].rearrange("p a b -> p (a b)"))
                ins.then_inc(sel_c, 1)
                after(22)
                for h in range(HEADS):
                    ins = dve.max_index(pos[:, h * TOP:h * TOP + TOP], f8[:, h, :], s64[:, h, :, :].rearrange("p a b -> p (a b)"))
                ins.then_inc(sel_c, 1)
                after(23)
                dve.tensor_scalar(j12[:, 0, :], pos[:], 3, None, ALU.logical_shift_right).then_inc(sel_c, 1)
                dve.tensor_scalar(j12[:, 1, :], pos[:], TOP - 1, None, ALU.bitwise_and).then_inc(sel_c, 1)
                after(25)
                dve.tensor_tensor(eq8[:], j12[:].unsqueeze(3).to_broadcast([P, 2, HK, TOP]),
                                  iota8[:].unsqueeze(1).unsqueeze(1).to_broadcast([P, 2, HK, TOP]),
                                  ALU.is_equal).then_inc(sel_c, 1)
                after(26)
                for s in range(2):
                    e = eq8[:, s, :, :].rearrange("p (h k) j -> p h k j", h=HEADS)
                    ins = dve.tensor_tensor(e, e, i8[:, :, s, :].unsqueeze(2).to_broadcast([P, HEADS, TOP, TOP]), ALU.mult)
                ins.then_inc(sel_c, 1)
                after(27)
                dve.tensor_reduce(i12[:], eq8[:], AX.X, ALU.add).then_inc(sel_c, 1)
                after(28)
                dve.tensor_scalar(clamp[:], i12[:, 0, :], float(STEPS), float(P - 1), ALU.is_ge, ALU.mult)
                dve.tensor_scalar(raw[:, 0, :], i12[:, 0, :], float(STEPS - 1), tq[:, 0:1], ALU.min, ALU.add)
                dve.tensor_scalar(raw[:, 2, :], f8[:].rearrange("p h k -> p (h k)"), 0.0, None, ALU.max).then_inc(sel_c, 1)
                after(29)
                dve.tensor_tensor(raw[:, 1, :], i12[:, 1, :], clamp[:], ALU.max).then_inc(sel_c, 1)
                after(30)
                dve.transpose(raw_t, raw[:].rearrange("p a b -> p (a b)")).then_inc(sel_c, 1)
                after(31)
                dve.tensor_copy(part[:, 0, :], raw_t[:, 2 * NG:3 * NG])
                dve.tensor_copy(pick[:, par, t, 0:2, :], raw_t[:, 0:2 * NG].rearrange("p (a b) -> p a b", a=2)).then_inc(sel_c, 1)
                after(32)
                dve.tensor_tensor(rest[:, 0, :], raw_t[:, 2 * NG:3 * NG], part[:, 0, :], ALU.subtract)
                dve.tensor_copy(pick[:, par, t, 2, :], part[:, 0, :]).then_inc(sel_c, 1)
                after(33)
                dve.tensor_copy(part[:, 1, :], rest[:, 0, :]).then_inc(split_c, 1)
                held(dve, "dve", split_c, q * 2 + 1)
                dve.tensor_tensor(rest[:, 1, :], rest[:, 0, :], part[:, 1, :], ALU.subtract)
                dve.tensor_copy(pick[:, par, t, 3, :], part[:, 1, :]).then_inc(split_c, 1)
                held(dve, "dve", split_c, q * 2 + 2)
                dve.tensor_copy(pick[:, par, t, 4, :], rest[:, 1, :]).then_inc(picked, 1)

            raw_t = s64[:, 2:4, :, :].rearrange("p a b c -> p (a b c)")[:, 0:3 * NG]

            def one_hots(gb, b, half, par, t):
                held(dve, "dve", hot1_done, gb)
                held(dve, "dve", g_mm, gb - 1 if not isinstance(gb, int) else max(0, gb - 1))
                cols = TG * HALF
                dve.tensor_tensor(hot1_eq[:], iota1[:, half, :].unsqueeze(1).to_broadcast([P, GB, cols]),
                                  pick[:, par, t, 0, b * GB:b * GB + GB].unsqueeze(2).to_broadcast([P, GB, cols]),
                                  ALU.is_equal).then_inc(hot1_eqd, 1)
                dve.tensor_tensor(hot2[:, b % 2, :, :], iota2[:].unsqueeze(1).to_broadcast([P, GB, P]),
                                  pick[:, par, t, 1, b * GB:b * GB + GB].unsqueeze(2).to_broadcast([P, GB, P]),
                                  ALU.is_equal).then_inc(hot2_done, 1)

            def mult(S, j, i1):
                held(dve, "dve", silu_done, S + 1)
                dve.tensor_tensor(act[:, j % 2, :], act[:, j % 2, :], G[:, i1, :], ALU.mult).then_inc(mult_done, 1)

            def select_whole(q, par, t):
                sel_norm(q)
                x_low(q, par, t)
                q_low(q)
                best(q, 0)
                best(q, 1)
                merge(q, par, t)

            for q in range(NT):
                select_whole(q, 0, q)
            dve.wait_ge(picked, NT)
            for t in range(NT):
                for b in range(NB):
                    one_hots(t * NB + b, b, 0, 0, t)

            def run_a(it, n, p, t):
                first = isinstance(it, int)
                q = NT if first else dve.snap(n * NT + NT + t)
                q_par = 1 if first else 1 - p
                i1 = 0 if isinstance(t, int) else t * PER
                held(dve, "dve", g_out, it * NB + NT * NB)
                for b in range(NB):
                    if b == 0:
                        sel_norm(q)
                    one_hots(it * NB + NT * NB + b, b, 1, p, t)
                    if b == 0:
                        x_low(q, q_par, t)
                    mult(it * PER + b, b, i1 + b)
                    if b == 0:
                        q_low(q)
                    if b == 1:
                        best(q, 0)
                    if b == 2:
                        best(q, 1)
                    if b == 3:
                        merge(q, q_par, t)

            def run_b(it, n, p, t, attn):
                r = dve.snap((n - LAG) * NT + t) if attn else None
                held(dve, "dve", picked, n * NT + NT + t + 1)
                held(dve, "dve", g_out, it * NB + NT * NB)
                for b in range(NB):
                    if attn and b == 0:
                        held(dve, "dve", xa_in, r * 16 + 16)
                        held(dve, "dve", a_out, r * 16 + 16)
                        normalise(xa, xaln, stata, att_c, r * ATT, arstd_done, r)
                    one_hots(it * NB + NT * NB + b, b, 0, 1 - p, t)
                    mult(it * PER + b, b, t * PER + (HALF + b))
                    if attn and b == 2:
                        held(dve, "dve", a_du, r * 2 + 2)
                        held(dve, "dve", a_y, r + 1)
                        dve.tensor_tensor(xaln[:], ps_s[:], xaln[:], ALU.add).then_inc(a_fin, 1)

            run_a(0, 0, 0, 0)

            def body(n, p, attn):
                iterations(dve, n, p, attn, run_a, run_b)
                held(dve, "dve", up_done, n * STEPS + STEPS)
                held(dve, "dve", res_in, n * 16 + 16)
                for t in range(NT):
                    dve.scalar_tensor_tensor(out=yres[:, t, :], in0=ps_out[t][:], scalar=0.5, in1=yres[:, t, :],
                                             op0=ALU.mult, op1=ALU.add).then_inc(evac_done, 1)

            stages(dve, body)

        @block.tensor
        def _(pe):
            def three(out, lhs, rhs, first, last, **kw):
                ins = None
                for k, (a, b) in enumerate(((H, H), (H, L), (L, H))):
                    ins = pe.matmul(out, lhs(a), rhs(b), start=first and k == 0, stop=last and k == 2, **kw)
                return ins

            pe.wait_ge(consts, 1)
            pe.wait_ge(small_in, 16 * 7)
            for h in range(HEADS):
                ins = pe.transpose(ps_s[:, h * P:h * P + P], G[:, KC, h * P:h * P + P], ident[:])
            ins.then_inc(k_tr, 1)
            pe.wait_ge(k_l, 3)
            pe.matmul(ps_s[0:RANK, 0:LEVELS * 4], ones[:, 0:RANK], xa[0:1, 0:LEVELS * 4], start=True, stop=True).then_inc(a_pe, 1)
            pe.wait_ge(a_out, 16)
            pe.matmul(ps_g[:].rearrange("p g q i -> p (g q i)"), ones, xs[0:1, :], start=True, stop=True).then_inc(a_pe, 1)
            pe.wait_ge(fly, 2 + 4 * LEVELS)
            at = 0 if LEVELS % 2 == 0 else 2
            pe.transpose(ps_s[0:RANK, 0:RANK], xaT[0:RANK, at, 0:RANK], ident[0:RANK, 0:RANK]).then_inc(a_pe, 1)
            pe.wait_ge(a_cp, 2)
            pe.matmul(ps_s[0:RANK, 0:RANK], xaT[0:RANK, 1, 0:RANK], xaT[0:RANK, 3, 0:RANK], start=True, stop=True).then_inc(a_pe, 1)
            pe.wait_ge(a_cp, 3)
            pe.matmul(ps_s[0:RANK, :], xaT[0:RANK, 2, 0:RANK], xaln[0:RANK, :], start=True, stop=True).then_inc(a_pe, 1)

            def w_transpose(i, j):
                held(pe, "pe", raw_in[j], i * 32 + 32)
                held(pe, "pe", w_l, i * PER + j - 1 if not isinstance(i, int) else max(0, j - 1))
                for c in range(KC):
                    ins = pe.transpose(ps_hd[j % 2][:, c * P:c * P + P], G[:, 8 + j, c * P:c * P + P], ident[:])
                ins.then_inc(w_tr, 1)

            for j in range(PER):
                w_transpose(0, j)
            with pe.Fori(1, STEPS // PER) as i:
                for j in range(PER):
                    w_transpose(i, j)

            def transposes(q, atts):
                held(pe, "pe", sel_c, q * SEL + 4)
                held(pe, "pe", s_simc, q * 2)
                held(pe, "pe", a_fin, atts + 1)
                for c in range(KC):
                    ins = pe.transpose(ps_s[:, c * P:c * P + P], xln[:, c * P:c * P + P], ident[:])
                ins.then_inc(s_t, 1)

            def queries(q, par, t):
                held(pe, "pe", s_xl, q + 1)
                for h in range(HEADS):
                    for c in range(KC):
                        ins = three(ps_s[:, h * P:h * P + P], lambda a: wq[:, a, c, h * P:h * P + P],
                                    lambda b: xT[:, par, b, c, ds(t * P, P)], c == 0, c == KC - 1)
                ins.then_inc(s_q, 1)

            def scores(q, h2):
                if h2 == 0:
                    held(pe, "pe", s_ql, q + 1)
                else:
                    held(pe, "pe", s_simc, q * 2 + 1)
                for h in range(2):
                    ins = three(ps_s[:, h * 2 * NK:(h + 1) * 2 * NK],
                                lambda a: qT[:, a, (2 * h2 + h) * P:(2 * h2 + h) * P + P],
                                lambda b: kb[:, b, 2 * h2 + h, :], True, True)
                ins.then_inc(s_sim, 1)

            def g_batch(gb, b):
                held(pe, "pe", hot2_done, gb + 1)
                held(pe, "pe", hot1_done, gb + 1)
                held(pe, "pe", g_out, gb)
                for g in range(GB):
                    for k in range(3):
                        ins = pe.matmul(ps_g[:, g, :, :].rearrange("p q i -> p (q i)"), hot2[:, b % 2, g, :], hot1[:, b % 2, k, g, :],
                                        start=k == 0, stop=k == 2)
                ins.then_inc(g_mm, 1)

            def down(it, j, par):
                held(pe, "pe", wd_in[j % 2], it * 32 + (j // 2) * 16 + 16)
                S = it * PER + j
                held(pe, "pe", silu_done, S - 1 if not isinstance(S, int) else max(0, S - 1))
                for c in range(KC):
                    ins = three(ps_hd[j % 2][:], lambda a: wd[:, j % 2, a * D + c * P:a * D + c * P + P],
                                lambda b: xT[:, par, b, c, :], c == 0, c == KC - 1)
                ins.then_inc(down_done, 1)

            def up(it, j):
                held(pe, "pe", wu_in[j % 2], it * 32 - 32 + (j // 2) * 16 + 16)
                held(pe, "pe", hidl_done, it * PER - PER + j + 1)
                for t in range(NT):
                    ins = three(ps_out[t][:], lambda a: hid[:, j, a, t * P:t * P + P],
                                lambda b: wu[:, j % 2, b * D:b * D + D], False, False, skip_group_check=True)
                ins.then_inc(up_done, 1)

            def clear_out():
                for t in range(NT):
                    pe.matmul(ps_out[t][:], zer[:, 0:P], zer[:], start=True, stop=True, skip_group_check=True)

            pe.wait_ge(a_fin, 1)
            for q in range(NT):
                transposes(q, 0)
                queries(q, 0, q)
                scores(q, 0)
                scores(q, 1)
            for t in range(NT):
                for b in range(NB):
                    g_batch(t * NB + b, b)
            clear_out()

            def run_a(it, n, p, t, atts):
                first = isinstance(it, int)
                q = NT if first else pe.snap(n * NT + NT + t)
                q_par = 1 if first else 1 - p
                for b in range(NB):
                    if not first:
                        up(it, b)
                    if b == 0:
                        transposes(q, atts)
                    if b == 1:
                        scores(q, 0)
                    down(it, b, p)
                    g_batch(it * NB + NT * NB + b, b)
                    if b == 0:
                        queries(q, q_par, t)
                    if b == 1:
                        scores(q, 1)

            def run_b(it, n, p, t, attn):
                r = pe.snap((n - LAG) * NT + t) if attn else None
                for b in range(NB):
                    up(it, b)
                    if attn and b == 1:
                        held(pe, "pe", att_c, r * ATT + 4)
                        held(pe, "pe", s_simc, n * (2 * NT) + 4 * NT)
                        held(pe, "pe", a_fin, r + 1)
                        for c in range(KC):
                            ins = pe.transpose(ps_s[:, c * P:c * P + P], xaln[:, c * P:c * P + P], ident[:])
                        ins.then_inc(a_t, 1)
                    if attn and b == 2:
                        held(pe, "pe", a_zc, r + 1)
                        pe.matmul(ps_s[:], zT[:], M[:], start=True, stop=True).then_inc(a_y, 1)
                    down(it, b, p)
                    g_batch(it * NB + NT * NB + b, b)
                    if attn and b == 1:
                        held(pe, "pe", a_x, r + 1)
                        for c in range(KC):
                            ins = pe.matmul(ps_s[0:RANK, 0:P], wb[:, c, :], xaT[:, c, :], start=c == 0, stop=c == KC - 1)
                        ins.then_inc(a_z, 1)

            run_a(0, 0, 0, 0, 0)

            def body(n, p, attn):
                before = (n - LAG) * NT if attn else None
                with pe.Fori(1, NT) as t:
                    run_a(pe.snap(n * ITERS + t), n, p, t, before if attn else atts_done[0])
                with pe.Fori(0, NT) as t:
                    run_b(pe.snap(n * ITERS + NT + t), n, p, t, attn)
                run_a(pe.snap(n * ITERS + ITERS), n + 1, 1 - p, 0, before + NT if attn else atts_done[0])
                held(pe, "pe", evac_done, n * NT + NT)
                clear_out()

            atts_done = [0]

            def body_counted(n, p, attn):
                body(n, p, attn)
                if attn:
                    atts_done[0] = NT * NBLK

            stages(pe, body_counted)


_INS = {"u": "L0_attn_u", "A_factors": "L0_attn_A_factors", "W_b_rank": "L0_attn_W_b_rank", "W_b_state": "L0_attn_W_b_state",
        "W_c_rank": "L0_attn_W_c_rank", "W_c_model": "L0_attn_W_c_model", "D_vec": "L0_attn_D_vec", "Wq": "L0_ffn_Wq",
        "keys": "L0_ffn_keys", "e_down": "L0_ffn_e_down", "e_up": "L0_ffn_e_up"}


def kernel(**inputs):
    import numpy as _np
    import concourse.bacc as _bacc
    from concourse import mybir as _mybir
    from concourse.bass_utils import run_bass_kernel_spmd as _run

    nc = _bacc.Bacc("TRN2", target_bir_lowering=False, num_devices=1)
    arrays, args = {}, []
    for short, name in _INS.items():
        a = _np.ascontiguousarray(inputs[name])
        arrays[f"in_{short}"] = a
        args.append(nc.dram_tensor(f"in_{short}", a.shape, _mybir.dt.from_np(a.dtype), kind="ExternalInput").ap())
    shape = inputs["L0_attn_u"].shape
    blocks = shape[0] * shape[1] // 512
    y = nc.dram_tensor("y_all", (2 * blocks, 4, 128, shape[2]), _mybir.dt.float32, kind="ExternalOutput").ap()
    macaron(nc, *args, y)
    r = _run(nc, [arrays], core_ids=[0])
    return r.results[0]["y_all"][blocks:].reshape(shape)
```

```python
from contextlib import ExitStack

import concourse.bass as bass
from concourse import mybir

F32 = mybir.dt.float32
F32R = mybir.dt.float32r
BF16 = mybir.dt.bfloat16
U32 = mybir.dt.uint32
ALU = mybir.AluOpType
ACT = mybir.ActivationFunctionType
AX = mybir.AxisListType
ds = bass.ds

P = 128
H, L = 0, 1


def macaron(nc, u, A_factors, W_b_rank, W_b_state, W_c_rank, W_c_model, D_vec, Wq, keys, e_down, e_up, y_all):
    D = u.shape[2]
    NTOK = u.shape[0] * u.shape[1]
    BLK = 512
    NT = BLK // P
    NBLK = NTOK // BLK
    KC = D // P
    HEADS, NK, _, DK = keys.shape
    TOP = 8
    HK = HEADS * TOP
    E = e_down.shape[0]
    STEPS = E // P
    HALF = STEPS // 2
    RANK = W_b_rank.shape[1]
    LEVELS = A_factors.shape[0]
    EPS = 1e-5
    NG = 32
    TG = P // NG
    GB = 8
    NB = NG // GB
    PER = 4
    ITERS = STEPS // PER
    SETS = STEPS // PER
    RAW0, TR0 = HALF, HALF + 8
    NSTAGE = 2 * NBLK
    LAG = 2
    assert NK == P and HK == 32 and 2 * DK == P and TG * HK == P and NB == PER and BLK == 512 and D == 512

    u_t = u.rearrange("b (t p) d -> b t p d", p=P)
    x_in = nc.dram_tensor("x_in", (NSTAGE + 2, NT, P, D), F32, kind="Internal").ap()
    wd_dram = nc.dram_tensor("wd_t", (STEPS + 2, P, D), F32, kind="Internal").ap()
    ed_t = e_down.rearrange("(s p) d -> p s d", p=P)
    wu_dram = nc.dram_tensor("wu_copy", (STEPS, P, D), F32, kind="Internal").ap()

    with ExitStack() as ctx:
        def sb(name, shape, dt=F32):
            return ctx.enter_context(nc.sbuf_tensor(name, shape, dt))

        def sem(name):
            return ctx.enter_context(nc.semaphore(name))

        G = sb("G", [P, STEPS, BLK])
        wd = sb("wd", [P, 2, 2 * D], F32R)
        wu = sb("wu", [P, 2, 2 * D], F32R)
        xT = sb("xT", [P, 2, 2, KC, BLK], F32R)
        act = sb("act", [P, 2, BLK])
        hid = sb("hid", [P, PER, 2, BLK], F32R)
        wq = sb("wq", [P, 2, KC, HEADS * P], F32R)
        kb = sb("kb", [P, 2, HEADS, 2 * NK], F32R)
        pick = sb("pick", [P, 2, NT, 5, NG])
        hot1 = sb("hot1", [P, 2, 3, GB, TG * HALF], BF16)
        hot1_eq = sb("hot1_eq", [P, GB, TG * HALF], BF16)
        hot2 = sb("hot2", [P, 2, GB, P], BF16)
        xs = sb("xs", [P, D])
        xln = sb("xln", [P, D])
        qT = sb("qT", [P, 2, HEADS * P], F32R)
        sims = sb("sims", [P, 2, 2, NK])
        yres = sb("yres", [P, NT, D])
        xa = sb("xa", [P, D])
        xaln = sb("xaln", [P, D])
        xaT = sb("xaT", [P, KC, P])
        zT = sb("zT", [RANK, P])
        M = sb("M", [RANK, D])
        wb = sb("wb", [P, KC, RANK])
        Dv = sb("Dv", [P, D])
        v8 = sb("v8", [P, HEADS, 2, TOP])
        i8 = sb("i8", [P, HEADS, 2, TOP], U32)
        s64 = sb("s64", [P, HEADS, TOP, TOP])
        f8 = sb("f8", [P, HEADS, TOP])
        pos = sb("pos", [P, HK], U32)
        j12 = sb("j12", [P, 2, HK], U32)
        eq8 = sb("eq8", [P, 2, HK, TOP], BF16)
        i12 = sb("i12", [P, 2, HK])
        clamp = sb("clamp", [P, HK])
        raw = sb("raw", [P, 3, HK])
        rest = sb("rest", [P, 2, HK])
        part = sb("part", [P, 2, HK], BF16)
        stat = sb("stat", [P, 12])
        stata = sb("stata", [P, 12])
        iota1 = sb("iota1", [P, 2, TG * HALF], BF16)
        iota2 = sb("iota2", [P, P], BF16)
        iota8 = sb("iota8", [P, TOP], BF16)
        tq = sb("tq", [P, 1])
        nhalf = sb("nhalf", [P, 1])
        ident = sb("ident", [P, P])
        zer = sb("zer", [P, D], BF16)
        ones = s64[0:1, 0:2, :, :].rearrange("p a b c -> p (a b c)")

        ps_out = [ctx.enter_context(nc.psum_tensor(f"ps_out{t}", [P, D], F32)) for t in range(NT)]
        ps_hd = [ctx.enter_context(nc.psum_tensor(f"ps_hd{t}", [P, BLK], F32)) for t in range(2)]
        ps_s = ctx.enter_context(nc.psum_tensor("ps_s", [P, 512], F32))
        ps_g = ctx.enter_context(nc.psum_tensor("ps_g", [P, GB, TG, HALF], F32))

        consts = sem("consts")
        tq_set = sem("tq_set")
        const_c = sem("const_c")
        small_in = sem("small_in")
        fac_in = sem("fac_in")
        x_copied = sem("x_copied")
        up_copied = sem("up_copied")
        raw_in = [sem(f"raw_in{j}") for j in range(2)]
        w_tr = sem("w_tr")
        w_cp = [sem(f"w_cp{j}") for j in range(2)]
        w_out = [sem(f"w_out{j}") for j in range(2)]
        k_tr = sem("k_tr")
        k_h = sem("k_h")
        k_l = sem("k_l")
        fly = sem("fly")
        a_pe = sem("a_pe")
        a_cp = sem("a_cp")
        wd_in = [sem(f"wd_in{j}") for j in range(2)]
        wu_in = [sem(f"wu_in{j}") for j in range(2)]
        wd_h = sem("wd_h")
        wd_l = sem("wd_l")
        wu_h = sem("wu_h")
        wu_l = sem("wu_l")
        down_done = sem("down_done")
        silu_done = sem("silu_done")
        mult_done = sem("mult_done")
        hidh_done = sem("hidh_done")
        hidl_done = sem("hidl_done")
        up_done = sem("up_done")
        evac_done = sem("evac_done")
        res_in = sem("res_in")
        block_out = sem("block_out")
        hot2_done = sem("hot2_done")
        hot1_eqd = sem("hot1_eqd")
        hot1_done = sem("hot1_done")
        g_mm = sem("g_mm")
        g_out = sem("g_out")
        x_in_s = sem("x_in_s")
        norm_c = sem("norm_c")
        sel_c = sem("sel_c")
        rstd_done = sem("rstd_done")
        s_t = sem("s_t")
        s_xh = sem("s_xh")
        s_xl = sem("s_xl")
        s_q = sem("s_q")
        s_qh = sem("s_qh")
        s_ql = sem("s_ql")
        s_sim = sem("s_sim")
        s_simc = sem("s_simc")
        split_c = sem("split_c")
        picked = sem("picked")
        xa_in = sem("xa_in")
        att_c = sem("att_c")
        arstd_done = sem("arstd_done")
        a_t = sem("a_t")
        a_x = sem("a_x")
        a_z = sem("a_z")
        a_zc = sem("a_zc")
        a_y = sem("a_y")
        a_du = sem("a_du")
        a_fin = sem("a_fin")
        a_out = sem("a_out")
        apart = {n: sem(f"apart_{n}") for n in ("sp", "act", "dve", "pool", "pe")}
        block = ctx.enter_context(nc.Block())

        def held(eng, name, s, value):
            if isinstance(value, int):
                if value > 0:
                    eng.wait_ge(s, value)
                return
            eng.wait_ge(s, value)
            eng.sem_inc(apart[name], 1)

        def stages(eng, body):
            for n0, n1, attn in ((0, LAG, False), (LAG, NBLK + LAG, True), (NBLK + LAG, NSTAGE, False)):
                with eng.Fori(0, (n1 - n0) // 2) as m:
                    with eng.Fori(0, 2) as p:
                        body(eng.snap(m * 2 + p + n0), p, attn)

        def iterations(eng, n, p, attn, run_a, run_b, between=None):
            with eng.Fori(1, NT) as t:
                run_a(eng.snap(n * ITERS + t), n, p, t)
            if between:
                between(n)
            with eng.Fori(0, NT) as t:
                run_b(eng.snap(n * ITERS + NT + t), n, p, t, attn)
            run_a(eng.snap(n * ITERS + ITERS), n + 1, 1 - p, 0)

        def iterations_ahead(eng, n, p, attn, run_a, run_b):
            with eng.Fori(1, NT - 1) as t:
                run_a(eng.snap(n * ITERS + t), n, p, t, (p, t + 1))
            run_a(eng.snap(n * ITERS + NT - 1), n, p, NT - 1, (1 - p, 0))
            run_b(eng.snap(n * ITERS + NT), n, p, 0, attn, (1 - p, 1))
            with eng.Fori(1, NT - 1) as t:
                run_b(eng.snap(n * ITERS + NT + t), n, p, t, attn, (1 - p, t + 1))
            run_b(eng.snap(n * ITERS + NT + NT - 1), n, p, NT - 1, attn, (1 - p, 0))
            run_a(eng.snap(n * ITERS + ITERS), n + 1, 1 - p, 0, (1 - p, 1))

        SEL_IDX0, SEL_IDX1, SEL = 8, 16, 29
        NORM = 4
        ATT = 4


        @block.sync
        def _(sp):
            sp.dma_start(G[:, 0:KC, :], Wq.rearrange("(c p) n -> p c n", p=P)).then_inc(small_in, 16)
            sp.dma_start(G[:, KC, :], keys.rearrange("h k s d -> k h (s d)")).then_inc(small_in, 16)
            sp.dma_start(wb[:], W_b_rank.rearrange("(c p) r -> p c r", p=P)).then_inc(small_in, 16)
            sp.dma_start(xaT[0:RANK, 0, 0:RANK], W_b_state).then_inc(small_in, 16)
            sp.dma_start(xaT[0:RANK, 1, 0:RANK], W_c_rank).then_inc(small_in, 16)
            sp.dma_start(xaln[0:RANK, :], W_c_model).then_inc(small_in, 16)
            sp.dma_start(xa[0:1, 0:LEVELS * 4], A_factors.rearrange("(o l) a b -> o (l a b)", o=1)).then_inc(small_in, 16)
            sp.dma_start(G[0:1, KC + 1, :], D_vec.rearrange("(o d) -> o d", o=1)).then_inc(a_out, 16)

            def raw_load(i, k):
                if not isinstance(i, int) or i > 0:
                    held(sp, "sp", w_tr, (i * 2 + k - 2) * PER + PER)
                sp.dma_start(G[:, RAW0 + k * PER:RAW0 + k * PER + PER, :],
                             ed_t[:, ds((i * 2 + k) * PER, PER), :]).then_inc(raw_in[k], 16)

            def first_loads(q):
                held(sp, "sp", s_t, q)
                sp.dma_start(xs[:], u_t[0, q]).then_inc(x_in_s, 16)
                for k in range(2):
                    raw_load(q, k)

            first_loads(0)
            first_loads(1)
            with sp.Fori(2, NT) as q:
                first_loads(q)
            sp.wait_ge(s_t, NT)
            sp.wait_ge(x_copied, 16 * NT)
            sp.dma_start(xs[:], x_in[1, 0]).then_inc(x_in_s, 16)
            for k in range(2):
                sp.wait_ge(w_out[k], 16 * (SETS // 2 + 1 - k))

            def load_down(it, j, step):
                held(sp, "sp", down_done, it * PER + j - 1 if not isinstance(it, int) else max(0, it * PER + j - 1))
                sp.dma_start(wd[:, j % 2, D:2 * D].bitcast(F32), wd_dram[step]).then_inc(wd_in[j % 2], 16)

            def load_up(it, j, step):
                held(sp, "sp", up_done, (it - 1) * PER + j - 1)
                sp.dma_start(wu[:, j % 2, D:2 * D].bitcast(F32), wu_dram[step]).then_inc(wu_in[j % 2], 16)

            sp.wait_ge(up_copied, 16 * NT)
            load_down(0, 0, 0)
            load_down(0, 1, 1)
            for j in range(2):
                sp.dma_start(wu[:, j, D:2 * D].bitcast(F32), wu_dram[j]).then_inc(wu_in[j], 16)
            sp.wait_ge(s_t, NT + 1)
            sp.dma_start(xs[:], x_in[1, 1]).then_inc(x_in_s, 16)
            load_down(0, 2, 2)
            load_down(0, 3, 3)
            load_down(1, 0, PER)
            load_down(1, 1, PER + 1)

            def stream(it, up0, down0, next_up):
                for j in range(PER):
                    if j < 2:
                        load_up(it, j + 2, up0 + j + 2)
                        load_down(it, j + 2, down0 + j + 2)
                    else:
                        load_up(it + 1, j - 2, next_up + j - 2)
                        load_down(it + 1, j - 2, down0 + j + 2)

            def run_a(it, n, p, t):
                held(sp, "sp", s_t, n * NT + NT + t + 1)
                if isinstance(t, int):
                    sp.dma_start(xs[:], x_in[n + 1, 1]).then_inc(x_in_s, 16)
                    stream(it, STEPS - PER, 0, 0)
                else:
                    with_next = sp.snap(n * NT + NT + t + 1)
                    sp.dma_start(xs[:], x_in.rearrange("s t p d -> (s t) p d")[with_next]).then_inc(x_in_s, 16)
                    stream(it, t * PER - PER, t * PER, t * PER)

            def run_b(it, n, p, t, attn):
                if attn:
                    r = (n - LAG) * NT + t
                    held(sp, "sp", a_fin, r + 1)
                    sp.dma_start(xa[:], y_all.rearrange("s t p d -> (s t) p d")[sp.snap((n - LAG) * NT + t)]).then_inc(xa_in, 16)
                stream(it, HALF - PER + t * PER, HALF + t * PER, HALF + t * PER)

            def residual(n):
                held(sp, "sp", block_out, n * 16 + 16)
                sp.dma_start(yres[:], x_in[n].rearrange("t p d -> p t d")).then_inc(res_in, 16)

            for n0, n1, attn in ((0, LAG, False), (LAG, NBLK + LAG, True), (NBLK + LAG, NSTAGE, False)):
                if n0 == NBLK + LAG:
                    sp.wait_ge(a_out, 16 + 16 * NT * NBLK)
                with sp.Fori(0, (n1 - n0) // 2) as m:
                    with sp.Fori(0, 2) as p:
                        n = sp.snap(m * 2 + p + n0)
                        if attn:
                            held(sp, "sp", a_out, n * (16 * NT) - (LAG * 16 * NT - 16))
                        iterations(sp, n, p, attn, run_a, run_b, residual)
            sp.wait_ge(block_out, 16 * (NSTAGE + 1))
            for j in range(2):
                sp.wait_ge(wd_in[j], 16 * (STEPS * NSTAGE // 2 + 3))
                sp.wait_ge(wu_in[j], 16 * (STEPS * NSTAGE // 2 + 1))
            sp.wait_ge(x_in_s, 16 * (NT * (NSTAGE + 1) + 2))

        @block.gpsimd
        def _(pool):
            def mark(ins):
                ins.then_inc(const_c, 1)

            mark(pool.memset(ident[:], 0.0))
            mark(pool.memset(zer[:], 0.0))
            mark(pool.memset(ones, 1.0))
            mark(pool.memset(nhalf[:], -0.5))
            for h in range(2):
                mark(pool.iota(iota1[:, h, :], pattern=[[HK, TG], [1, HALF]], base=HALF * h, channel_multiplier=0,
                               allow_small_or_imprecise_dtypes=True))
            mark(pool.iota(iota2[:], pattern=[[1, P]], base=0, channel_multiplier=0, allow_small_or_imprecise_dtypes=True))
            mark(pool.iota(iota8[:], pattern=[[1, TOP]], base=0, channel_multiplier=0, allow_small_or_imprecise_dtypes=True))
            mark(pool.memset(kb[:].bitcast(F32), 0.0))
            pool.wait_ge(const_c, 9)
            pool.affine_select(out=ident[:], in_=ident[:], compare_op=ALU.not_equal, fill=1.0, base=0,
                               pattern=[[-1, P]], channel_multiplier=1).then_inc(consts, 1)

            def rstd(q):
                held(pool, "pool", norm_c, q * NORM + 3)
                pool.tensor_tensor(stat[:, 8:9], stat[:, 7:8], nhalf[:], ALU.pow).then_inc(rstd_done, 1)

            def arstd(r):
                held(pool, "pool", att_c, r * ATT + 3)
                pool.tensor_tensor(stata[:, 8:9], stata[:, 7:8], nhalf[:], ALU.pow).then_inc(arstd_done, 1)

            def hot1_scores(gb, b, par, t):
                held(pool, "pool", g_mm, gb - 1 if not isinstance(gb, int) else max(0, gb - 1))
                held(pool, "pool", hot1_eqd, gb + 1)
                pool.tensor_tensor(hot1[:, b % 2, :, :, :], hot1_eq[:].unsqueeze(1).to_broadcast([P, 3, GB, TG * HALF]),
                                   pick[:, par, t, 2:5, b * GB:b * GB + GB].unsqueeze(3).to_broadcast(
                                       [P, 3, GB, TG * HALF]), ALU.mult).then_inc(hot1_done, 1)

            def hid_low(S, j):
                held(pool, "pool", hidh_done, S + 1)
                pool.tensor_tensor(hid[:, j, L, :], act[:, j % 2, :], hid[:, j, H, :].bitcast(F32),
                                   ALU.subtract).then_inc(hidl_done, 1)

            def up_weights_low(number, slot):
                held(pool, "pool", wu_h, number + 1)
                w = wu[:, slot, :]
                pool.tensor_tensor(w[:, D:2 * D], w[:, D:2 * D].bitcast(F32), w[:, 0:D].bitcast(F32), ALU.subtract).then_inc(wu_l, 1)

            def first_batches(q):
                held(pool, "pool", picked, q)
                for b in range(NB):
                    hot1_scores((q - 1) * NB + b, b, 0, q - 1)

            rstd(0)
            rstd(1)
            first_batches(1)
            rstd(2)
            with pool.Fori(2, NT) as q:
                first_batches(q)
                rstd(q + 1)
            first_batches(NT)
            hot1_scores(NT * NB, 0, 0, 0)

            def run_a(it, n, p, t, nxt):
                first = isinstance(it, int)
                for b in range(NB):
                    if b or not first:
                        hid_low(it * PER + b - 1, (b - 1) % PER)
                    if not first:
                        up_weights_low(it * PER - PER + b + 1, (b + 1) % 2)
                    if b + 1 < NB:
                        hot1_scores(it * NB + NT * NB + b + 1, b + 1, p, t)
                    else:
                        hot1_scores(it * NB + NT * NB + NB, 0, *nxt)
                    if b == 1:
                        rstd(n * NT + NT + t + 1)
                if first:
                    up_weights_low(0, 0)

            def run_b(it, n, p, t, attn, nxt):
                r = pool.snap((n - LAG) * NT + t) if attn else None
                for b in range(NB):
                    hid_low(it * PER + b - 1, (b - 1) % PER)
                    up_weights_low(it * PER - PER + b + 1, (b + 1) % 2)
                    if b + 1 < NB:
                        hot1_scores(it * NB + NT * NB + b + 1, b + 1, 1 - p, t)
                    else:
                        hot1_scores(it * NB + NT * NB + NB, 0, *nxt)
                    if attn and b == 0:
                        arstd(r)
                    if attn and b == 1:
                        held(pool, "pool", a_t, r + 1)
                        pool.tensor_tensor(xaln[:], xaln[:], Dv[:], ALU.mult).then_inc(a_du, 1)
                        held(pool, "pool", a_du, r * 2 + 1)
                        pool.tensor_tensor(xaln[:], xaln[:], xa[:], ALU.add).then_inc(a_du, 1)

            run_a(0, 0, 0, 0, (0, 1))
            stages(pool, lambda n, p, attn: iterations_ahead(pool, n, p, attn, run_a, run_b))

        @block.scalar
        def _(sc):
            sc.preload_act_table(ACT.Silu)
            sc.wait_ge(small_in, 16 * 7)
            sc.copy(wq[:, H, :, :], G[:, 0:KC, :]).then_inc(k_h, 1)
            sc.wait_ge(k_tr, 1)
            for s in range(2):
                rows = slice(DK * s, DK * s + DK)
                sc.copy(kb[rows, H, :, s * NK:s * NK + NK],
                        ps_s[rows, :].rearrange("p (h k) -> p h k", h=HEADS)).then_inc(k_h, 1)
            def set_copy(i, k):
                held(sc, "act", w_out[k], 0 if isinstance(i, int) and i == 0 else i * 16 + (16 if k == 0 else 0))
                for j in range(0, PER, 2):
                    held(sc, "act", w_tr, (i * 2 + k) * PER + j + 1)
                    sc.copy(G[:, TR0 + k * PER + j, :], ps_hd[0][:]).then_inc(w_cp[0], 1)
                held(sc, "act", w_cp[0], (i * 2 + k) * 2 + 2)
                held(sc, "act", w_cp[1], (i * 2 + k) * 2 + 2)
                sc.dma_start(wd_dram[ds((i * 2 + k) * PER, PER)].rearrange("s p d -> p s d"),
                             G[:, TR0 + k * PER:TR0 + k * PER + PER, :]).then_inc(w_out[k], 16)

            def weights_high(w, landed, done, slot, use):
                held(sc, "act", landed[slot], use * 16)
                sc.copy(w[:, slot, 0:D], w[:, slot, D:2 * D].bitcast(F32)).then_inc(done, 1)

            def x_high(q, par, t):
                held(sc, "act", s_t, q + 1)
                sc.copy(xT[:, par, H, :, ds(t * P, P)], ps_s[:].rearrange("p (c n) -> p c n", c=KC)).then_inc(s_xh, 1)

            def q_high(q):
                sc.wait_ge(s_q, q + 1)
                sc.copy(qT[:, H, :], ps_s[:]).then_inc(s_qh, 1)

            def sim_copy(q, h2):
                free = q * SEL + (SEL_IDX0 if h2 else SEL_IDX1 - SEL)
                held(sc, "act", sel_c, max(0, free) if isinstance(free, int) else free)
                held(sc, "act", s_sim, q * 2 + h2 + 1)
                sc.copy(sims[:].rearrange("p a b c -> p (a b c)"), ps_s[:]).then_inc(s_simc, 1)

            def g_evac(gb, b, half, t):
                held(sc, "act", g_mm, gb + 1)
                view = G[:, half * HALF:half * HALF + HALF, :].rearrange("p i (a q g) -> p i a q g", a=NT, q=TG)
                sc.copy(view[:, :, t, :, b * GB:b * GB + GB].rearrange("p i q g -> p g q i"), ps_g[:]).then_inc(g_out, 1)

            def silu(S, j):
                held(sc, "act", hidl_done, S - 1 if not isinstance(S, int) else max(0, S - 1))
                held(sc, "act", down_done, S + 1)
                sc.activation(act[:, j % 2, :], ps_hd[j % 2][:], ACT.Silu).then_inc(silu_done, 1)

            def hid_high(S, j):
                sc.wait_ge(mult_done, S + 1)
                sc.copy(hid[:, j, H, :], act[:, j % 2, :]).then_inc(hidh_done, 1)

            def first(q):
                batch = lambda b: None if isinstance(q, int) and q == 0 else g_evac((q - 1) * NB + b, b, 0, q - 1)
                x_high(q, 0, q)
                set_copy(q, 0)
                batch(0)
                q_high(q)
                batch(1)
                set_copy(q, 1)
                if isinstance(q, int) and q == 0:
                    sc.wait_ge(w_out[0], 16)
                    sc.dma_start(wd_dram[STEPS:STEPS + 2].rearrange("s p d -> p s d"), G[:, TR0:TR0 + 2, :]).then_inc(w_out[0], 16)
                sc.dma_start(x_in[ds(q * (NBLK // NT), NBLK // NT)], u_t[ds(q * (NBLK // NT), NBLK // NT)]).then_inc(x_copied, 16)
                sc.dma_start(wu_dram[ds(q * (STEPS // NT), STEPS // NT)],
                             e_up.rearrange("(s p) d -> s p d", p=P)[ds(q * (STEPS // NT), STEPS // NT)]).then_inc(up_copied, 16)
                sim_copy(q, 0)
                batch(2)
                sim_copy(q, 1)
                batch(3)

            first(0)
            first(1)
            with sc.Fori(2, NT) as q:
                first(q)
            for b in range(NB):
                g_evac((NT - 1) * NB + b, b, 0, NT - 1)
            sc.dma_start(x_in[NSTAGE:NSTAGE + 2], u_t[0:2]).then_inc(block_out, 16)
            weights_high(wd, wd_in, wd_h, 0, 1)

            def next_up_high(it, b):
                if not isinstance(it, int):
                    weights_high(wu, wu_in, wu_h, (b + 1) % 2, it * 2 - 2 + (b + 1) // 2 + 1)
                elif b == PER - 1:
                    weights_high(wu, wu_in, wu_h, 0, 1)

            def next_down_high(it, b):
                weights_high(wd, wd_in, wd_h, (b + 1) % 2, it * 2 + (b + 1) // 2 + 1)

            def run_a(it, n, p, t):
                first = isinstance(it, int)
                q = 4 if first else sc.snap(n * NT + NT + t)
                q_par = 1 if first else 1 - p
                held(sc, "act", mult_done, it * PER)
                for b in range(NB):
                    if b or not first:
                        hid_high(it * PER + b - 1, (b - 1) % PER)
                    if b == 0:
                        x_high(q, q_par, t)
                    next_up_high(it, b)
                    next_down_high(it, b)
                    if b == 0:
                        q_high(q)
                    if b == 1:
                        sim_copy(q, 1)
                    silu(it * PER + b, b)
                    g_evac(it * NB + NT * NB + b, b, 1, t)
                    if b == 0:
                        sim_copy(q, 0)

            def run_b(it, n, p, t, attn):
                r = sc.snap((n - LAG) * NT + t) if attn else None
                held(sc, "act", mult_done, it * PER)
                for b in range(NB):
                    hid_high(it * PER + b - 1, (b - 1) % PER)
                    next_up_high(it, b)
                    if attn and b == 1:
                        sc.wait_ge(a_t, r + 1)
                        sc.copy(xaT[:].rearrange("p c n -> p (c n)"), ps_s[:]).then_inc(a_x, 1)
                    if attn and b == 2:
                        sc.wait_ge(a_z, r + 1)
                        sc.copy(zT[:], ps_s[0:RANK, 0:P]).then_inc(a_zc, 1)
                    next_down_high(it, b)
                    silu(it * PER + b, b)
                    g_evac(it * NB + NT * NB + b, b, 0, t)
                    if attn and b == 3:
                        held(sc, "act", a_fin, r + 2)
                        sc.dma_start(x_in.rearrange("s t p d -> (s t) p d")[sc.snap((n - LAG + NBLK) * NT + t)],
                                     xaln[:]).then_inc(a_out, 16)

            run_a(0, 0, 0, 0)

            def body(n, p, attn):
                iterations(sc, n, p, attn, run_a, run_b)
                held(sc, "act", evac_done, n * NT + NT)
                sc.dma_start(y_all[n].rearrange("t p d -> p t d"), yres[:]).then_inc(block_out, 16)

            stages(sc, body)
            sc.wait_ge(a_out, 16 + 16 * NT * NBLK)
            sc.wait_ge(x_copied, 16 * NT)

        @block.vector
        def _(dve):
            for t in range(TG):
                dve.memset(tq[NG * t:NG * t + NG, :], float(HK * t)).then_inc(tq_set, 1)
            dve.wait_ge(tq_set, TG)
            dve.wait_ge(consts, 1)
            dve.wait_ge(small_in, 16 * 7)
            dve.wait_ge(k_h, 1)
            dve.tensor_tensor(wq[:, L, :, :], G[:, 0:KC, :], wq[:, H, :, :].bitcast(F32), ALU.subtract).then_inc(k_l, 1)
            dve.wait_ge(k_h, 3)
            for s in range(2):
                rows = slice(DK * s, DK * s + DK)
                dve.tensor_tensor(kb[rows, L, :, s * NK:s * NK + NK], ps_s[rows, :].rearrange("p (h k) -> p h k", h=HEADS),
                                  kb[rows, H, :, s * NK:s * NK + NK].bitcast(F32), ALU.subtract).then_inc(k_l, 1)
            dve.wait_ge(a_pe, 1)
            dve.tensor_copy(stata[0:RANK, 0:12], ps_s[0:RANK, 0:12]).then_inc(fly, 1)
            dve.tensor_copy(stat[0:RANK, 0:12], ps_s[0:RANK, 12:24]).then_inc(fly, 1)
            c = 2

            def factor(lvl, i, j):
                at = lvl * 4 + i * 2 + j
                return stata[0:RANK, at:at + 1] if at < 12 else stat[0:RANK, at - 12:at - 11]

            for lvl in range(LEVELS):
                src = xaT[0:RANK, 0 if lvl % 2 == 0 else 2, 0:RANK].rearrange("r (a i b) -> r a i b", a=2 ** lvl, i=2)
                dst = xaT[0:RANK, 2 if lvl % 2 == 0 else 0, 0:RANK].rearrange("r (a i b) -> r a i b", a=2 ** lvl, i=2)
                dve.wait_ge(fly, c)
                for j in range(2):
                    dve.tensor_scalar(dst[:, :, j, :], src[:, :, 0, :], factor(lvl, 0, j), None, ALU.mult).then_inc(fly, 1)
                c += 2
                dve.wait_ge(fly, c)
                for j in range(2):
                    dve.scalar_tensor_tensor(out=dst[:, :, j, :], in0=src[:, :, 1, :], scalar=factor(lvl, 1, j),
                                             in1=dst[:, :, j, :], op0=ALU.mult, op1=ALU.add).then_inc(fly, 1)
                c += 2
            dve.wait_ge(a_pe, 2)
            dve.tensor_copy(Dv[:], ps_g[:].rearrange("p g q i -> p (g q i)")).then_inc(a_cp, 1)
            dve.wait_ge(a_pe, 3)
            dve.tensor_copy(xaT[0:RANK, 3, 0:RANK], ps_s[0:RANK, 0:RANK]).then_inc(a_cp, 1)
            dve.wait_ge(a_pe, 4)
            dve.tensor_copy(xaT[0:RANK, 2, 0:RANK], ps_s[0:RANK, 0:RANK]).then_inc(a_cp, 1)
            dve.wait_ge(a_pe, 5)
            dve.tensor_copy(M[:], ps_s[0:RANK, :]).then_inc(a_fin, 1)

            def set_copy(i, k):
                held(dve, "dve", w_out[k], 0 if isinstance(i, int) and i == 0 else i * 16 + (16 if k == 0 else 0))
                for j in range(1, PER, 2):
                    held(dve, "dve", w_tr, (i * 2 + k) * PER + j + 1)
                    dve.tensor_copy(G[:, TR0 + k * PER + j, :], ps_hd[1][:]).then_inc(w_cp[1], 1)

            def down_weights_low(number, slot):
                held(dve, "dve", wd_h, number + 1)
                w = wd[:, slot, :]
                dve.tensor_tensor(w[:, D:2 * D], w[:, D:2 * D].bitcast(F32), w[:, 0:D].bitcast(F32), ALU.subtract).then_inc(wd_l, 1)

            def normalise(x, out, st, chain, base, done, number):
                dve.bn_stats(st[:, 0:6], x[:]).then_inc(chain, 1)
                held(dve, "dve", chain, base + 1)
                dve.bn_aggr(st[:, 6:8], st[:, 0:6]).then_inc(chain, 1)
                held(dve, "dve", chain, base + 2)
                dve.tensor_scalar(st[:, 7:8], st[:, 7:8], EPS, None, ALU.add).then_inc(chain, 1)
                held(dve, "dve", done, number + 1)
                dve.tensor_scalar(out[:], x[:], st[:, 6:7], st[:, 8:9], ALU.subtract, ALU.mult).then_inc(chain, 1)

            def sel_norm(q):
                held(dve, "dve", x_in_s, q * 16 + 16)
                held(dve, "dve", s_t, q)
                normalise(xs, xln, stat, norm_c, q * NORM, rstd_done, q)

            def x_low(q, par, t):
                held(dve, "dve", s_xh, q + 1)
                dve.tensor_tensor(xT[:, par, L, :, ds(t * P, P)], ps_s[:].rearrange("p (c n) -> p c n", c=KC),
                                  xT[:, par, H, :, ds(t * P, P)].bitcast(F32), ALU.subtract).then_inc(s_xl, 1)

            def q_low(q):
                held(dve, "dve", s_qh, q + 1)
                dve.tensor_tensor(qT[:, L, :], ps_s[:], qT[:, H, :].bitcast(F32), ALU.subtract).then_inc(s_ql, 1)

            def best(q, h2):
                held(dve, "dve", s_simc, q * 2 + h2 + 1)
                for h in range(2):
                    for s in range(2):
                        dve.max(v8[:, 2 * h2 + h, s, :], sims[:, h, s, :]).then_inc(sel_c, 1)
                held(dve, "dve", sel_c, q * SEL + 8 * h2 + 4)
                for h in range(2):
                    for s in range(2):
                        dve.max_index(i8[:, 2 * h2 + h, s, :], v8[:, 2 * h2 + h, s, :], sims[:, h, s, :]).then_inc(sel_c, 1)

            def merge_sums(q):
                def after(k):
                    held(dve, "dve", sel_c, q * SEL + k)

                after(16)
                dve.tensor_tensor(s64[:], v8[:, :, 0, :].unsqueeze(3).to_broadcast([P, HEADS, TOP, TOP]),
                                  v8[:, :, 1, :].unsqueeze(2).to_broadcast([P, HEADS, TOP, TOP]), ALU.add).then_inc(sel_c, 1)
                after(17)
                for h in range(HEADS):
                    ins = dve.max(f8[:, h, :], s64[:, h, :, :].rearrange("p a b -> p (a b)"))
                ins.then_inc(sel_c, 1)
                after(18)
                for h in range(HEADS):
                    ins = dve.max_index(pos[:, h * TOP:h * TOP + TOP], f8[:, h, :], s64[:, h, :, :].rearrange("p a b -> p (a b)"))
                ins.then_inc(sel_c, 1)

            def merge_experts(q):
                def after(k):
                    held(dve, "dve", sel_c, q * SEL + k)

                after(19)
                dve.tensor_scalar(j12[:, 0, :], pos[:], 3, None, ALU.logical_shift_right).then_inc(sel_c, 1)
                dve.tensor_scalar(j12[:, 1, :], pos[:], TOP - 1, None, ALU.bitwise_and).then_inc(sel_c, 1)
                after(21)
                dve.tensor_tensor(eq8[:], j12[:].unsqueeze(3).to_broadcast([P, 2, HK, TOP]),
                                  iota8[:].unsqueeze(1).unsqueeze(1).to_broadcast([P, 2, HK, TOP]),
                                  ALU.is_equal).then_inc(sel_c, 1)
                after(22)
                for s in range(2):
                    e = eq8[:, s, :, :].rearrange("p (h k) j -> p h k j", h=HEADS)
                    ins = dve.tensor_tensor(e, e, i8[:, :, s, :].unsqueeze(2).to_broadcast([P, HEADS, TOP, TOP]), ALU.mult)
                ins.then_inc(sel_c, 1)
                after(23)
                dve.tensor_reduce(i12[:], eq8[:], AX.X, ALU.add).then_inc(sel_c, 1)

            def merge_layout(q, par, t):
                def after(k):
                    held(dve, "dve", sel_c, q * SEL + k)

                after(24)
                dve.tensor_scalar(clamp[:], i12[:, 0, :], float(STEPS), float(P - 1), ALU.is_ge, ALU.mult)
                dve.tensor_scalar(raw[:, 0, :], i12[:, 0, :], float(STEPS - 1), tq[:, 0:1], ALU.min, ALU.add)
                dve.tensor_scalar(raw[:, 2, :], f8[:].rearrange("p h k -> p (h k)"), 0.0, None, ALU.max).then_inc(sel_c, 1)
                after(25)
                dve.tensor_tensor(raw[:, 1, :], i12[:, 1, :], clamp[:], ALU.max).then_inc(sel_c, 1)
                after(26)
                dve.transpose(raw_t, raw[:].rearrange("p a b -> p (a b)")).then_inc(sel_c, 1)
                after(27)
                dve.tensor_copy(part[:, 0, :], raw_t[:, 2 * NG:3 * NG])
                dve.tensor_copy(pick[:, par, t, 0:2, :], raw_t[:, 0:2 * NG].rearrange("p (a b) -> p a b", a=2)).then_inc(sel_c, 1)
                after(28)
                dve.tensor_tensor(rest[:, 0, :], raw_t[:, 2 * NG:3 * NG], part[:, 0, :], ALU.subtract)
                dve.tensor_copy(pick[:, par, t, 2, :], part[:, 0, :]).then_inc(sel_c, 1)
                after(29)
                dve.tensor_copy(part[:, 1, :], rest[:, 0, :]).then_inc(split_c, 1)
                held(dve, "dve", split_c, q * 2 + 1)
                dve.tensor_tensor(rest[:, 1, :], rest[:, 0, :], part[:, 1, :], ALU.subtract)
                dve.tensor_copy(pick[:, par, t, 3, :], part[:, 1, :]).then_inc(split_c, 1)
                held(dve, "dve", split_c, q * 2 + 2)
                dve.tensor_copy(pick[:, par, t, 4, :], rest[:, 1, :]).then_inc(picked, 1)

            raw_t = s64[:, 2:4, :, :].rearrange("p a b c -> p (a b c)")[:, 0:3 * NG]

            def one_hots(gb, b, half, par, t):
                held(dve, "dve", hot1_done, gb)
                held(dve, "dve", g_mm, gb - 1 if not isinstance(gb, int) else max(0, gb - 1))
                cols = TG * HALF
                dve.tensor_tensor(hot1_eq[:], iota1[:, half, :].unsqueeze(1).to_broadcast([P, GB, cols]),
                                  pick[:, par, t, 0, b * GB:b * GB + GB].unsqueeze(2).to_broadcast([P, GB, cols]),
                                  ALU.is_equal).then_inc(hot1_eqd, 1)
                dve.tensor_tensor(hot2[:, b % 2, :, :], iota2[:].unsqueeze(1).to_broadcast([P, GB, P]),
                                  pick[:, par, t, 1, b * GB:b * GB + GB].unsqueeze(2).to_broadcast([P, GB, P]),
                                  ALU.is_equal).then_inc(hot2_done, 1)

            def mult(S, j, i1):
                held(dve, "dve", silu_done, S + 1)
                dve.tensor_tensor(act[:, j % 2, :], act[:, j % 2, :], G[:, i1, :], ALU.mult).then_inc(mult_done, 1)

            def first(q):
                batch = lambda b: None if isinstance(q, int) and q == 0 else one_hots((q - 1) * NB + b, b, 0, 0, q - 1)
                x_low(q, 0, q)
                batch(0)
                set_copy(q, 0)
                batch(1)
                q_low(q)
                batch(2)
                set_copy(q, 1)
                batch(3)
                best(q, 0)
                best(q, 1)
                sel_norm(q + 1)
                merge_sums(q)
                merge_experts(q)
                merge_layout(q, 0, q)

            sel_norm(0)
            first(0)
            first(1)
            with dve.Fori(2, NT) as q:
                first(q)
            for b in range(NB):
                one_hots((NT - 1) * NB + b, b, 0, 0, NT - 1)
            one_hots(NT * NB, 0, 1, 0, 0)
            down_weights_low(0, 0)

            def run_a(it, n, p, t, nxt):
                first = isinstance(it, int)
                q = NT if first else dve.snap(n * NT + NT + t)
                q_par = 1 if first else 1 - p
                tile0 = isinstance(t, int) and t == 0
                tile3 = isinstance(t, int) and t == NT - 1
                i1 = 0 if tile0 else t * PER
                gb = it * NB + NT * NB
                x_low(q, q_par, t)
                one_hots(gb + 1, 1, 1, p, t)
                down_weights_low(it * PER + 1, 1)
                if not tile0:
                    merge_sums(q - 1)
                    merge_experts(q - 1)
                    merge_layout(q - 1, q_par, t - 1)
                q_low(q)
                held(dve, "dve", g_out, gb)
                mult(it * PER, 0, i1)

                one_hots(gb + 2, 2, 1, p, t)
                best(q, 0)
                down_weights_low(it * PER + 2, 0)
                mult(it * PER + 1, 1, i1 + 1)
                sel_norm(q + 1)

                one_hots(gb + 3, 3, 1, p, t)
                down_weights_low(it * PER + 3, 1)
                best(q, 1)
                mult(it * PER + 2, 2, i1 + 2)

                if tile0 and not first:
                    evacuate(n - 1)
                    down_weights_low(it * PER + 4, 0)
                    mult(it * PER + 3, 3, i1 + 3)
                    one_hots(gb + 4, 0, 1, *nxt)
                else:
                    one_hots(gb + 4, 0, 0 if tile3 else 1, *nxt)
                    down_weights_low(it * PER + 4, 0)
                    mult(it * PER + 3, 3, i1 + 3)

            def run_b(it, n, p, t, attn, nxt):
                r = dve.snap((n - LAG) * NT + t) if attn else None
                tile3 = isinstance(t, int) and t == NT - 1
                gb = it * NB + NT * NB
                for b in range(NB):
                    if b + 1 < NB:
                        one_hots(gb + b + 1, b + 1, 0, 1 - p, t)
                    else:
                        one_hots(gb + b + 1, 0, 1 if tile3 else 0, *nxt)
                    down_weights_low(it * PER + b + 1, (b + 1) % 2)
                    if b == 0:
                        held(dve, "dve", g_out, gb)
                    mult(it * PER + b, b, t * PER + (HALF + b))
                    if attn and b == 0:
                        held(dve, "dve", xa_in, r * 16 + 16)
                        held(dve, "dve", a_out, r * 16 + 16)
                        normalise(xa, xaln, stata, att_c, r * ATT, arstd_done, r)
                    if b == 1 and isinstance(t, int) and t == 0:
                        merge_sums(n * NT + NT + NT - 1)
                        merge_experts(n * NT + NT + NT - 1)
                        merge_layout(n * NT + NT + NT - 1, 1 - p, NT - 1)
                    if attn and b == 2:
                        held(dve, "dve", a_du, r * 2 + 2)
                        held(dve, "dve", a_y, r + 1)
                        dve.tensor_tensor(xaln[:], ps_s[:], xaln[:], ALU.add).then_inc(a_fin, 1)

            def evacuate(n):
                held(dve, "dve", up_done, n * STEPS + STEPS)
                held(dve, "dve", res_in, n * 16 + 16)
                for tile in range(NT):
                    dve.scalar_tensor_tensor(out=yres[:, tile, :], in0=ps_out[tile][:], scalar=0.5, in1=yres[:, tile, :],
                                             op0=ALU.mult, op1=ALU.add).then_inc(evac_done, 1)

            run_a(0, 0, 0, 0, (0, 1))
            stages(dve, lambda n, p, attn: iterations_ahead(dve, n, p, attn, run_a, run_b))

        @block.tensor
        def _(pe):
            def three(out, lhs, rhs, first, last, **kw):
                ins = None
                for k, (a, b) in enumerate(((H, H), (H, L), (L, H))):
                    ins = pe.matmul(out, lhs(a), rhs(b), start=first and k == 0, stop=last and k == 2, **kw)
                return ins

            pe.wait_ge(consts, 1)
            pe.wait_ge(small_in, 16 * 7)
            for h in range(HEADS):
                ins = pe.transpose(ps_s[:, h * P:h * P + P], G[:, KC, h * P:h * P + P], ident[:])
            ins.then_inc(k_tr, 1)
            pe.wait_ge(k_l, 3)
            pe.matmul(ps_s[0:RANK, 0:LEVELS * 4], ones[:, 0:RANK], xa[0:1, 0:LEVELS * 4], start=True, stop=True).then_inc(a_pe, 1)
            pe.wait_ge(a_out, 16)
            pe.matmul(ps_g[:].rearrange("p g q i -> p (g q i)"), ones, G[0:1, KC + 1, :], start=True, stop=True).then_inc(a_pe, 1)
            pe.wait_ge(fly, 2 + 4 * LEVELS)
            at = 0 if LEVELS % 2 == 0 else 2
            pe.transpose(ps_s[0:RANK, 0:RANK], xaT[0:RANK, at, 0:RANK], ident[0:RANK, 0:RANK]).then_inc(a_pe, 1)
            pe.wait_ge(a_cp, 2)
            pe.matmul(ps_s[0:RANK, 0:RANK], xaT[0:RANK, 1, 0:RANK], xaT[0:RANK, 3, 0:RANK], start=True, stop=True).then_inc(a_pe, 1)
            pe.wait_ge(a_cp, 3)
            pe.matmul(ps_s[0:RANK, :], xaT[0:RANK, 2, 0:RANK], xaln[0:RANK, :], start=True, stop=True).then_inc(a_pe, 1)

            def w_transpose(i, k):
                held(pe, "pe", raw_in[k], i * 16 + 16)
                for j in range(PER):
                    held(pe, "pe", w_cp[j % 2], (i * 2 + k) * 2 + j // 2)
                    for c in range(KC):
                        ins = pe.transpose(ps_hd[j % 2][:, c * P:c * P + P], G[:, RAW0 + k * PER + j, c * P:c * P + P], ident[:])
                    ins.then_inc(w_tr, 1)

            def transposes(q, atts):
                held(pe, "pe", norm_c, q * NORM + 4)
                held(pe, "pe", s_simc, q * 2)
                held(pe, "pe", a_fin, atts + 1)
                for c in range(KC):
                    ins = pe.transpose(ps_s[:, c * P:c * P + P], xln[:, c * P:c * P + P], ident[:])
                ins.then_inc(s_t, 1)

            def queries(q, par, t):
                held(pe, "pe", s_xl, q + 1)
                for h in range(HEADS):
                    for c in range(KC):
                        ins = three(ps_s[:, h * P:h * P + P], lambda a: wq[:, a, c, h * P:h * P + P],
                                    lambda b: xT[:, par, b, c, ds(t * P, P)], c == 0, c == KC - 1)
                ins.then_inc(s_q, 1)

            def scores(q, h2):
                if h2 == 0:
                    held(pe, "pe", s_ql, q + 1)
                else:
                    held(pe, "pe", s_simc, q * 2 + 1)
                for h in range(2):
                    ins = three(ps_s[:, h * 2 * NK:(h + 1) * 2 * NK],
                                lambda a: qT[:, a, (2 * h2 + h) * P:(2 * h2 + h) * P + P],
                                lambda b: kb[:, b, 2 * h2 + h, :], True, True)
                ins.then_inc(s_sim, 1)

            def g_batch(gb, b):
                held(pe, "pe", hot2_done, gb + 1)
                held(pe, "pe", hot1_done, gb + 1)
                held(pe, "pe", g_out, gb)
                for g in range(GB):
                    for k in range(3):
                        ins = pe.matmul(ps_g[:, g, :, :].rearrange("p q i -> p (q i)"), hot2[:, b % 2, g, :], hot1[:, b % 2, k, g, :],
                                        start=k == 0, stop=k == 2)
                ins.then_inc(g_mm, 1)

            def down(it, j, par):
                S = it * PER + j
                held(pe, "pe", wd_l, S + 1)
                held(pe, "pe", silu_done, S - 1 if not isinstance(S, int) else max(0, S - 1))
                for c in range(KC):
                    ins = three(ps_hd[j % 2][:], lambda a: wd[:, j % 2, a * D + c * P:a * D + c * P + P],
                                lambda b: xT[:, par, b, c, :], c == 0, c == KC - 1)
                ins.then_inc(down_done, 1)

            def up(it, j):
                held(pe, "pe", wu_l, it * PER - PER + j + 1)
                held(pe, "pe", hidl_done, it * PER - PER + j + 1)
                for t in range(NT):
                    ins = three(ps_out[t][:], lambda a: hid[:, j, a, t * P:t * P + P],
                                lambda b: wu[:, j % 2, b * D:b * D + D], False, False, skip_group_check=True)
                ins.then_inc(up_done, 1)

            def clear_out():
                for t in range(NT):
                    pe.matmul(ps_out[t][:], zer[:, 0:P], zer[:], start=True, stop=True, skip_group_check=True)

            pe.wait_ge(a_fin, 1)
            def first(q):
                batch = lambda b: None if isinstance(q, int) and q == 0 else g_batch((q - 1) * NB + b, b)
                transposes(q, 0)
                w_transpose(q, 0)
                batch(0)
                queries(q, 0, q)
                batch(1)
                w_transpose(q, 1)
                scores(q, 0)
                batch(2)
                scores(q, 1)
                batch(3)

            first(0)
            first(1)
            with pe.Fori(2, NT) as q:
                first(q)
            for b in range(NB):
                g_batch((NT - 1) * NB + b, b)
            clear_out()

            def run_a(it, n, p, t, atts):
                first = isinstance(it, int)
                q = NT if first else pe.snap(n * NT + NT + t)
                q_par = 1 if first else 1 - p
                for b in range(NB):
                    if b == 0:
                        transposes(q, atts)
                    if not first:
                        up(it, b)
                    if b == 0:
                        queries(q, q_par, t)
                    if b == 1:
                        scores(q, 1)
                    down(it, b, p)
                    g_batch(it * NB + NT * NB + b, b)
                    if b == 0:
                        scores(q, 0)

            def run_b(it, n, p, t, attn):
                r = pe.snap((n - LAG) * NT + t) if attn else None
                for b in range(NB):
                    up(it, b)
                    if attn and b == 1:
                        held(pe, "pe", att_c, r * ATT + 4)
                        held(pe, "pe", s_simc, n * (2 * NT) + 4 * NT)
                        held(pe, "pe", a_fin, r + 1)
                        for c in range(KC):
                            ins = pe.transpose(ps_s[:, c * P:c * P + P], xaln[:, c * P:c * P + P], ident[:])
                        ins.then_inc(a_t, 1)
                    if attn and b == 2:
                        held(pe, "pe", a_zc, r + 1)
                        pe.matmul(ps_s[:], zT[:], M[:], start=True, stop=True).then_inc(a_y, 1)
                    down(it, b, p)
                    g_batch(it * NB + NT * NB + b, b)
                    if attn and b == 1:
                        held(pe, "pe", a_x, r + 1)
                        for c in range(KC):
                            ins = pe.matmul(ps_s[0:RANK, 0:P], wb[:, c, :], xaT[:, c, :], start=c == 0, stop=c == KC - 1)
                        ins.then_inc(a_z, 1)

            run_a(0, 0, 0, 0, 0)

            def body(n, p, attn):
                before = (n - LAG) * NT if attn else None
                with pe.Fori(1, NT) as t:
                    run_a(pe.snap(n * ITERS + t), n, p, t, before if attn else atts_done[0])
                with pe.Fori(0, NT) as t:
                    run_b(pe.snap(n * ITERS + NT + t), n, p, t, attn)
                run_a(pe.snap(n * ITERS + ITERS), n + 1, 1 - p, 0, before + NT if attn else atts_done[0])
                held(pe, "pe", evac_done, n * NT + NT)
                clear_out()

            atts_done = [0]

            def body_counted(n, p, attn):
                body(n, p, attn)
                if attn:
                    atts_done[0] = NT * NBLK

            stages(pe, body_counted)


_INS = {"u": "L0_attn_u", "A_factors": "L0_attn_A_factors", "W_b_rank": "L0_attn_W_b_rank", "W_b_state": "L0_attn_W_b_state",
        "W_c_rank": "L0_attn_W_c_rank", "W_c_model": "L0_attn_W_c_model", "D_vec": "L0_attn_D_vec", "Wq": "L0_ffn_Wq",
        "keys": "L0_ffn_keys", "e_down": "L0_ffn_e_down", "e_up": "L0_ffn_e_up"}


def kernel(**inputs):
    import numpy as _np
    import concourse.bacc as _bacc
    from concourse import mybir as _mybir
    from concourse.bass_utils import run_bass_kernel_spmd as _run

    nc = _bacc.Bacc("TRN2", target_bir_lowering=False, num_devices=1)
    arrays, args = {}, []
    for short, name in _INS.items():
        a = _np.ascontiguousarray(inputs[name])
        arrays[f"in_{short}"] = a
        args.append(nc.dram_tensor(f"in_{short}", a.shape, _mybir.dt.from_np(a.dtype), kind="ExternalInput").ap())
    shape = inputs["L0_attn_u"].shape
    blocks = shape[0] * shape[1] // 512
    y = nc.dram_tensor("y_all", (2 * blocks, 4, 128, shape[2]), _mybir.dt.float32, kind="ExternalOutput").ap()
    macaron(nc, *args, y)
    r = _run(nc, [arrays], core_ids=[0])
    return r.results[0]["y_all"][blocks:].reshape(shape)
```

```python
from contextlib import ExitStack

import concourse.bass as bass
from concourse import mybir

F32 = mybir.dt.float32
F32R = mybir.dt.float32r
BF16 = mybir.dt.bfloat16
U32 = mybir.dt.uint32
ALU = mybir.AluOpType
ACT = mybir.ActivationFunctionType
AX = mybir.AxisListType
ds = bass.ds

P = 128
H, L = 0, 1


def macaron(nc, u, A_factors, W_b_rank, W_b_state, W_c_rank, W_c_model, D_vec, Wq, keys, e_down, e_up, y_all):
    D = u.shape[2]
    NTOK = u.shape[0] * u.shape[1]
    BLK = 512
    NT = BLK // P
    NBLK = NTOK // BLK
    KC = D // P
    HEADS, NK, _, DK = keys.shape
    TOP = 8
    HK = HEADS * TOP
    E = e_down.shape[0]
    STEPS = E // P
    HALF = STEPS // 2
    RANK = W_b_rank.shape[1]
    LEVELS = A_factors.shape[0]
    EPS = 1e-5
    NG = 32
    TG = P // NG
    GB = 8
    NB = NG // GB
    PER = 4
    ITERS = STEPS // PER
    SETS = STEPS // PER
    RAW0, TR0 = HALF, HALF + 8
    NSTAGE = 2 * NBLK
    LAG = 2
    assert NK == P and HK == 32 and 2 * DK == P and TG * HK == P and NB == PER and BLK == 512 and D == 512

    u_t = u.rearrange("b (t p) d -> b t p d", p=P)
    x_in = nc.dram_tensor("x_in", (NSTAGE + 1, NT, P, D), F32, kind="Internal").ap()
    wd_dram = nc.dram_tensor("wd_t", (STEPS + 2, P, D), F32, kind="Internal").ap()
    ed_t = e_down.rearrange("(s p) d -> p s d", p=P)
    eu_s = e_up.rearrange("(s p) d -> s p d", p=P)
    wu_dram = nc.dram_tensor("wu_copy", (STEPS, P, D), F32, kind="Internal").ap()

    with ExitStack() as ctx:
        def sb(name, shape, dt=F32):
            return ctx.enter_context(nc.sbuf_tensor(name, shape, dt))

        def sem(name):
            return ctx.enter_context(nc.semaphore(name))

        G = sb("G", [P, STEPS, BLK])
        wd = sb("wd", [P, 2, 2 * D], F32R)
        wu = sb("wu", [P, 2, 2 * D], F32R)
        xT = sb("xT", [P, 2, 2, KC, BLK], F32R)
        act = sb("act", [P, 2, BLK])
        hid = sb("hid", [P, PER, 2, BLK], F32R)
        wk = sb("wk", [P, 2, KC, HEADS * 2 * NK], F32R)
        xt = sb("xt", [P, 2, KC, P], F32R)
        pick = sb("pick", [P, 2, NT, 5, NG], BF16)
        hot1 = sb("hot1", [P, 2, 3, GB, TG * HALF], BF16)
        hot1_eq = sb("hot1_eq", [P, GB, TG * HALF], BF16)
        hot2 = sb("hot2", [P, 2, GB, P], BF16)
        xs = sb("xs", [P, D])
        yres = sb("yres", [P, NT, D])
        xa = sb("xa", [P, D])
        xaln = sb("xaln", [P, D])
        xaT = sb("xaT", [P, KC, P])
        zT = sb("zT", [RANK, P])
        M = sb("M", [RANK, D])
        wb = sb("wb", [P, KC, RANK])
        Dv = sb("Dv", [P, D])
        v8 = sb("v8", [P, HEADS, 2, TOP])
        i8 = sb("i8", [P, HEADS, 2, TOP], U32)
        s64 = sb("s64", [P, HEADS, TOP, TOP])
        f8 = sb("f8", [P, HEADS, TOP])
        pos = sb("pos", [P, HK], U32)
        j12 = sb("j12", [P, 2, HK], U32)
        eq8 = s64[:].bitcast(BF16).rearrange("p h a b -> p (h a b)").rearrange("p (s k j) -> p s k j", s=2, j=TOP)
        i12 = sb("i12", [P, 2, HK])
        clamp = sb("clamp", [P, HK])
        raw = sb("raw", [P, 3, HK])
        rest = sb("rest", [P, 2, HK])
        part = sb("part", [P, 2, HK], BF16)
        stat = sb("stat", [P, 12])
        stata = sb("stata", [P, 12])
        iota1 = sb("iota1", [P, 2, TG * HALF], BF16)
        iota2 = sb("iota2", [P, P], BF16)
        iota8 = sb("iota8", [P, TOP], BF16)
        tq = sb("tq", [P, 1])
        nhalf = sb("nhalf", [P, 1])
        ident = sb("ident", [P, P])
        zer = sb("zer", [P, P], BF16)
        wq_raw = G[:, 0:KC, :]
        keys_raw = G[:, KC, :]
        wqT = G[:, KC + 2:KC + 2 + HEADS, :]
        keysT = G[:, 2 * KC + 2:2 * KC + 4, :].rearrange("p a b -> p (a b)").rearrange("p (h k) -> p h k", h=HEADS)
        fw = G[0:RANK, 3 * KC:4 * KC, 0:RANK]
        ones = s64[0:1, 0:2, :, :].rearrange("p a b c -> p (a b c)")

        ps_out = [ctx.enter_context(nc.psum_tensor(f"ps_out{t}", [P, D], F32)) for t in range(NT)]
        ps_hd = [ctx.enter_context(nc.psum_tensor(f"ps_hd{t}", [P, BLK], F32)) for t in range(2)]
        ps_s = ctx.enter_context(nc.psum_tensor("ps_s", [P, 512], F32))
        ps_g = ctx.enter_context(nc.psum_tensor("ps_g", [P, GB, TG, HALF], F32))

        consts = sem("consts")
        tq_set = sem("tq_set")
        const_c = sem("const_c")
        small_in = sem("small_in")
        x_copied = sem("x_copied")
        up_copied = sem("up_copied")
        x_rest = sem("x_rest")
        up_rest = sem("up_rest")
        raw_in = [sem(f"raw_in{j}") for j in range(2)]
        w_tr = sem("w_tr")
        w_cp = sem("w_cp")
        w_out = [sem(f"w_out{j}") for j in range(2)]
        k_tr = sem("k_tr")
        k_set = sem("k_set")
        q_cp = [sem(f"q_cp{j}") for j in range(2)]
        wk_mm = sem("wk_mm")
        wk_h = sem("wk_h")
        wk_l = sem("wk_l")
        fly = sem("fly")
        a_pe = sem("a_pe")
        a_cp = sem("a_cp")
        wd_in = [sem(f"wd_in{j}") for j in range(2)]
        wu_in = [sem(f"wu_in{j}") for j in range(2)]
        wd_h = sem("wd_h")
        wd_l = sem("wd_l")
        wu_h = sem("wu_h")
        wu_l = sem("wu_l")
        down_done = sem("down_done")
        silu_done = sem("silu_done")
        mult_done = sem("mult_done")
        hidh_done = sem("hidh_done")
        hidl_done = sem("hidl_done")
        up_done = sem("up_done")
        evac_done = sem("evac_done")
        res_in = sem("res_in")
        block_out = sem("block_out")
        hot2_done = sem("hot2_done")
        hot1_eqd = sem("hot1_eqd")
        hot1_done = sem("hot1_done")
        g_mm = sem("g_mm")
        g_out = sem("g_out")
        x_in_s = sem("x_in_s")
        norm_c = sem("norm_c")
        sel_c = sem("sel_c")
        rstd_done = sem("rstd_done")
        s_t = sem("s_t")
        s_xh = sem("s_xh")
        s_xl = sem("s_xl")
        s_xt = sem("s_xt")
        s_sim = sem("s_sim")
        lay_c = sem("lay_c")
        split_c = sem("split_c")
        picked = sem("picked")
        xa_in = sem("xa_in")
        att_c = sem("att_c")
        arstd_done = sem("arstd_done")
        a_t = sem("a_t")
        a_x = sem("a_x")
        a_z = sem("a_z")
        a_zc = sem("a_zc")
        a_y = sem("a_y")
        a_du = sem("a_du")
        a_fin = sem("a_fin")
        a_out = sem("a_out")
        apart = {n: sem(f"apart_{n}") for n in ("sp", "act", "dve", "pool", "pe")}
        block = ctx.enter_context(nc.Block())

        def held(eng, name, s, value):
            if isinstance(value, int):
                if value > 0:
                    eng.wait_ge(s, value)
                return
            eng.wait_ge(s, value)
            eng.sem_inc(apart[name], 1)

        def reg(eng, value):
            return value if isinstance(value, int) else eng.snap(value)

        def stages(eng, body):
            for n0, n1, attn in ((0, LAG, False), (LAG, NBLK + LAG, True), (NBLK + LAG, NSTAGE - 2, False)):
                with eng.Fori(0, (n1 - n0) // 2) as m:
                    with eng.Fori(0, 2) as p:
                        body(eng.snap(m * 2 + p + n0), p, attn)
            for p in range(2):
                body(NSTAGE - 2 + p, p, False)

        def is_last(n):
            return isinstance(n, int) and n == NSTAGE - 1

        def selects(n):
            return not is_last(n)

        def iterations(eng, n, p, attn, run_a, run_b, run_last, between=None):
            with eng.Fori(1, NT) as t:
                run_a(eng.snap(n * ITERS + t), n, p, t)
            if between:
                between(n)
            with eng.Fori(0, NT) as t:
                run_b(eng.snap(n * ITERS + NT + t), n, p, t, attn)
            if is_last(n):
                run_last(n * ITERS + ITERS)
            else:
                run_a(reg(eng, n * ITERS + ITERS), n + 1, 1 - p, 0)

        def iterations_ahead(eng, n, p, attn, run_a, run_b, run_last):
            with eng.Fori(1, NT - 1) as t:
                run_a(eng.snap(n * ITERS + t), n, p, t, (p, t + 1))
            run_a(reg(eng, n * ITERS + NT - 1), n, p, NT - 1, None if is_last(n) else (1 - p, 0))
            run_b(reg(eng, n * ITERS + NT), n, p, 0, attn, (1 - p, 1))
            with eng.Fori(1, NT - 1) as t:
                run_b(eng.snap(n * ITERS + NT + t), n, p, t, attn, (1 - p, t + 1))
            run_b(reg(eng, n * ITERS + NT + NT - 1), n, p, NT - 1, attn, (1 - p, 0))
            if is_last(n):
                run_last(n * ITERS + ITERS)
            else:
                run_a(reg(eng, n * ITERS + ITERS), n + 1, 1 - p, 0, (1 - p, 1))

        SEL_IDX0, SEL_IDX1, SEL = 8, 16, 24
        LAY = 5
        NORM = 4
        ATT = 4


        @block.sync
        def _(sp):
            sp.dma_start(wq_raw, Wq.rearrange("(c p) n -> p c n", p=P)).then_inc(small_in, 16)
            sp.dma_start(keys_raw, keys.rearrange("h k s d -> k h (s d)")).then_inc(small_in, 16)
            sp.dma_start(wb[:], W_b_rank.rearrange("(c p) r -> p c r", p=P)).then_inc(small_in, 16)
            sp.dma_start(fw[:, 0, :], W_b_state).then_inc(small_in, 16)
            sp.dma_start(fw[:, 1, :], W_c_rank).then_inc(small_in, 16)
            sp.dma_start(xaln[0:RANK, :], W_c_model).then_inc(small_in, 16)
            sp.dma_start(xa[0:1, 0:LEVELS * 4], A_factors.rearrange("(o l) a b -> o (l a b)", o=1)).then_inc(small_in, 16)
            sp.dma_start(G[0:1, KC + 1, :], D_vec.rearrange("(o d) -> o d", o=1)).then_inc(a_out, 16)

            def raw_load(i, k):
                if not isinstance(i, int) or i > 0:
                    held(sp, "sp", w_tr, (i * 2 + k - 2) * PER + PER)
                sp.dma_start(G[:, RAW0 + k * PER:RAW0 + k * PER + PER, :],
                             ed_t[:, ds((i * 2 + k) * PER, PER), :]).then_inc(raw_in[k], 16)

            def first_loads(q):
                held(sp, "sp", s_t, q)
                sp.dma_start(xs[:], u_t[0, q]).then_inc(x_in_s, 16)
                for k in range(2):
                    raw_load(q, k)

            first_loads(0)
            first_loads(1)
            with sp.Fori(2, NT) as q:
                first_loads(q)
            sp.wait_ge(s_t, NT)
            sp.dma_start(xs[:], u_t[1, 0]).then_inc(x_in_s, 16)
            for k in range(2):
                sp.wait_ge(w_out[k], 16 * (SETS // 2 + 1 - k))

            def load_down(it, j, step):
                held(sp, "sp", down_done, it * PER + j - 1 if not isinstance(it, int) else max(0, it * PER + j - 1))
                sp.dma_start(wd[:, j % 2, D:2 * D].bitcast(F32), wd_dram[step]).then_inc(wd_in[j % 2], 16)

            def load_up(it, j, step):
                held(sp, "sp", up_done, (it - 1) * PER + j - 1)
                sp.dma_start(wu[:, j % 2, D:2 * D].bitcast(F32), wu_dram[step]).then_inc(wu_in[j % 2], 16)

            sp.wait_ge(x_copied, 16 * NT)
            sp.wait_ge(up_copied, 16 * NT)
            load_down(0, 0, 0)
            load_down(0, 1, 1)
            for j in range(2):
                sp.dma_start(wu[:, j, D:2 * D].bitcast(F32), wu_dram[j]).then_inc(wu_in[j], 16)
            sp.wait_ge(s_t, NT + 1)
            sp.dma_start(xs[:], u_t[1, 1]).then_inc(x_in_s, 16)
            load_down(0, 2, 2)
            load_down(0, 3, 3)
            load_down(1, 0, PER)
            load_down(1, 1, PER + 1)

            def stream(it, up0, down0, next_up):
                for j in range(PER):
                    if j < 2:
                        load_up(it, j + 2, up0 + j + 2)
                        load_down(it, j + 2, down0 + j + 2)
                    else:
                        load_up(it + 1, j - 2, next_up + j - 2)
                        load_down(it + 1, j - 2, down0 + j + 2)

            def run_a(it, n, p, t):
                if selects(n):
                    held(sp, "sp", s_t, n * NT + NT + t + 1)
                if isinstance(t, int):
                    if selects(n):
                        sp.dma_start(xs[:], x_in[n + 1, 1]).then_inc(x_in_s, 16)
                    stream(it, STEPS - PER, 0, 0)
                else:
                    if selects(n):
                        sp.dma_start(xs[:], x_in.rearrange("s t p d -> (s t) p d")[sp.snap(n * NT + NT + t + 1)]).then_inc(x_in_s, 16)
                    stream(it, t * PER - PER, t * PER, t * PER)

            def run_b(it, n, p, t, attn):
                if attn:
                    r = (n - LAG) * NT + t
                    held(sp, "sp", a_fin, r + 1)
                    sp.dma_start(xa[:], y_all.rearrange("s t p d -> (s t) p d")[sp.snap((n - LAG) * NT + t)]).then_inc(xa_in, 16)
                stream(it, HALF - PER + t * PER, HALF + t * PER, HALF + t * PER)

            def run_last(it):
                for j in range(2):
                    load_up(it, j + 2, STEPS - PER + j + 2)

            def residual(n):
                held(sp, "sp", block_out, n * 16 + 16)
                sp.dma_start(yres[:], x_in[n].rearrange("t p d -> p t d")).then_inc(res_in, 16)

            sp.wait_ge(up_rest, 16 * NT)

            seen = [False, False]

            def body(n, p, attn):
                if attn and not seen[0]:
                    sp.wait_ge(x_rest, 16 * 2)
                    seen[0] = True
                if seen[0] and not attn and not seen[1]:
                    sp.wait_ge(a_out, 16 + 16 * NT * NBLK)
                    seen[1] = True
                if attn:
                    held(sp, "sp", a_out, n * (16 * NT) - (LAG * 16 * NT - 16))
                iterations(sp, n, p, attn, run_a, run_b, run_last, residual)

            stages(sp, body)
            sp.wait_ge(block_out, 16 * (NSTAGE + 1))
            for j in range(2):
                sp.wait_ge(wd_in[j], 16 * (STEPS * NSTAGE // 2 + 1))
                sp.wait_ge(wu_in[j], 16 * (STEPS * NSTAGE // 2))
            sp.wait_ge(x_in_s, 16 * (NT * NSTAGE + 1))

        @block.gpsimd
        def _(pool):
            def mark(ins):
                ins.then_inc(const_c, 1)

            mark(pool.memset(ident[:], 0.0))
            mark(pool.memset(zer[:], 0.0))
            mark(pool.memset(ones, 1.0))
            mark(pool.memset(nhalf[:], -0.5))
            for h in range(2):
                mark(pool.iota(iota1[:, h, :], pattern=[[HK, TG], [1, HALF]], base=HALF * h, channel_multiplier=0,
                               allow_small_or_imprecise_dtypes=True))
            mark(pool.iota(iota2[:], pattern=[[1, P]], base=0, channel_multiplier=0, allow_small_or_imprecise_dtypes=True))
            mark(pool.iota(iota8[:], pattern=[[1, TOP]], base=0, channel_multiplier=0, allow_small_or_imprecise_dtypes=True))
            mark(pool.memset(G[:, 2 * KC + 2:2 * KC + 4, :], 0.0))
            pool.wait_ge(const_c, 9)
            pool.affine_select(out=ident[:], in_=ident[:], compare_op=ALU.not_equal, fill=1.0, base=0,
                               pattern=[[-1, P]], channel_multiplier=1).then_inc(consts, 1)

            def rstd(q):
                held(pool, "pool", norm_c, q * NORM + 3)
                pool.tensor_tensor(stat[:, 8:9], stat[:, 7:8], nhalf[:], ALU.pow).then_inc(rstd_done, 1)

            def arstd(r):
                held(pool, "pool", att_c, r * ATT + 3)
                pool.tensor_tensor(stata[:, 8:9], stata[:, 7:8], nhalf[:], ALU.pow).then_inc(arstd_done, 1)

            def hot1_scores(gb, b, par, t):
                held(pool, "pool", g_mm, gb - 1 if not isinstance(gb, int) else max(0, gb - 1))
                held(pool, "pool", hot1_eqd, gb + 1)
                pool.tensor_tensor(hot1[:, b % 2, :, :, :], hot1_eq[:].unsqueeze(1).to_broadcast([P, 3, GB, TG * HALF]),
                                   pick[:, par, t, 2:5, b * GB:b * GB + GB].unsqueeze(3).to_broadcast(
                                       [P, 3, GB, TG * HALF]), ALU.mult).then_inc(hot1_done, 1)

            def hid_low(S, j):
                held(pool, "pool", hidh_done, S + 1)
                pool.tensor_tensor(hid[:, j, L, :], act[:, j % 2, :], hid[:, j, H, :].bitcast(F32),
                                   ALU.subtract).then_inc(hidl_done, 1)

            def up_weights_low(number, slot):
                held(pool, "pool", wu_h, number + 1)
                w = wu[:, slot, :]
                pool.tensor_tensor(w[:, D:2 * D], w[:, D:2 * D].bitcast(F32), w[:, 0:D].bitcast(F32), ALU.subtract).then_inc(wu_l, 1)

            def first_batches(q):
                held(pool, "pool", picked, q)
                for b in range(NB):
                    hot1_scores((q - 1) * NB + b, b, 0, q - 1)
                    if b == 1 and not (isinstance(q, int) and q == NT):
                        rstd(q + 1)

            rstd(0)
            rstd(1)
            first_batches(1)
            with pool.Fori(2, NT) as q:
                first_batches(q)
            first_batches(NT)
            up_weights_low(0, 0)
            hot1_scores(NT * NB, 0, 0, 0)

            def run_a(it, n, p, t, nxt):
                first = isinstance(it, int) and it == 0
                for b in range(NB):
                    if b or not first:
                        hid_low(it * PER + b - 1, (b - 1) % PER)
                    if not first:
                        up_weights_low(it * PER - PER + b + 1, (b + 1) % 2)
                    if b + 1 < NB:
                        hot1_scores(it * NB + NT * NB + b + 1, b + 1, p, t)
                    elif nxt:
                        hot1_scores(it * NB + NT * NB + NB, 0, *nxt)
                    if b == 1 and selects(n):
                        rstd(n * NT + NT + t + 1)

            def run_b(it, n, p, t, attn, nxt):
                r = reg(pool, (n - LAG) * NT + t) if attn else None
                for b in range(NB):
                    hid_low(it * PER + b - 1, (b - 1) % PER)
                    up_weights_low(it * PER - PER + b + 1, (b + 1) % 2)
                    if attn and b == 0:
                        arstd(r)
                    if is_last(n):
                        continue
                    if b + 1 < NB:
                        hot1_scores(it * NB + NT * NB + b + 1, b + 1, 1 - p, t)
                    else:
                        hot1_scores(it * NB + NT * NB + NB, 0, *nxt)
                    if attn and b == 1:
                        held(pool, "pool", a_t, r + 1)
                        pool.tensor_tensor(xaln[:], xaln[:], Dv[:], ALU.mult).then_inc(a_du, 1)
                        held(pool, "pool", a_du, r * 2 + 1)
                        pool.tensor_tensor(xaln[:], xaln[:], xa[:], ALU.add).then_inc(a_du, 1)

            def run_last(it):
                hid_low(it * PER - 1, PER - 1)
                for b in range(PER - 1):
                    up_weights_low(it * PER - PER + b + 1, (b + 1) % 2)

            run_a(0, 0, 0, 0, (0, 1))
            stages(pool, lambda n, p, attn: iterations_ahead(pool, n, p, attn, run_a, run_b, run_last))

        @block.scalar
        def _(sc):
            sc.preload_act_table(ACT.Silu)
            sc.wait_ge(small_in, 16 * 7)
            sc.wait_ge(k_tr, 1)
            sc.wait_ge(consts, 1)
            for side in range(2):
                rows = slice(DK * side, DK * side + DK)
                sc.copy(keysT[rows, :, side * NK:side * NK + NK],
                        ps_s[rows, :].rearrange("p (h k) -> p h k", h=HEADS)).then_inc(k_set, 1)
            for h in range(0, HEADS, 2):
                sc.wait_ge(k_tr, h + 2)
                sc.copy(wqT[:, h, :], ps_out[h][:]).then_inc(q_cp[0], 1)
            for i in range(2 * KC):
                sc.wait_ge(wk_mm, i + 1)
                sc.copy(wk[:, H, i % KC, i // KC * 512:i // KC * 512 + 512], ps_out[i % NT][:]).then_inc(wk_h, 1)

            def set_copy(i, k):
                held(sc, "act", w_out[k], 0 if isinstance(i, int) and i == 0 else i * 16 + (16 if k == 0 else 0))
                for j in range(PER):
                    held(sc, "act", w_tr, (i * 2 + k) * PER + j + 1)
                    sc.copy(G[:, TR0 + k * PER + j, :], ps_hd[j % 2][:]).then_inc(w_cp, 1)
                held(sc, "act", w_cp, (i * 2 + k) * PER + PER)
                sc.dma_start(wd_dram[ds((i * 2 + k) * PER, PER)].rearrange("s p d -> p s d"),
                             G[:, TR0 + k * PER:TR0 + k * PER + PER, :]).then_inc(w_out[k], 16)

            def weights_high(w, landed, done, slot, use):
                held(sc, "act", landed[slot], use * 16)
                sc.copy(w[:, slot, 0:D], w[:, slot, D:2 * D].bitcast(F32)).then_inc(done, 1)

            def x_high(q):
                held(sc, "act", s_t, q + 1)
                sc.copy(xt[:, H, :, :], ps_s[:].rearrange("p (c n) -> p c n", c=KC)).then_inc(s_xh, 1)

            def x_place(q, par, t):
                held(sc, "act", s_xl, q + 1)
                sc.copy(xT[:, par, :, :, ds(t * P, P)], xt[:].bitcast(F32)).then_inc(s_xt, 1)

            def g_evac(gb, b, half, t):
                held(sc, "act", g_mm, gb + 1)
                view = G[:, half * HALF:half * HALF + HALF, :].rearrange("p i (a q g) -> p i a q g", a=NT, q=TG)
                sc.copy(view[:, :, t, :, b * GB:b * GB + GB].rearrange("p i q g -> p g q i"), ps_g[:]).then_inc(g_out, 1)

            def silu(S, j):
                held(sc, "act", hidl_done, S - 1 if not isinstance(S, int) else max(0, S - 1))
                held(sc, "act", down_done, S + 1)
                sc.activation(act[:, j % 2, :], ps_hd[j % 2][:], ACT.Silu).then_inc(silu_done, 1)

            def hid_high(S, j):
                sc.wait_ge(mult_done, S + 1)
                sc.copy(hid[:, j, H, :], act[:, j % 2, :]).then_inc(hidh_done, 1)

            def first(q):
                batch = lambda b: None if isinstance(q, int) and q == 0 else g_evac((q - 1) * NB + b, b, 0, q - 1)
                set_copy(q, 0)
                x_place(q, 0, q)
                set_copy(q, 1)
                if isinstance(q, int) and q == 0:
                    sc.wait_ge(w_out[0], 16)
                    sc.dma_start(wd_dram[STEPS:STEPS + 2].rearrange("s p d -> p s d"), G[:, TR0:TR0 + 2, :]).then_inc(w_out[0], 16)
                sc.dma_start(x_in[ds(q, 1)], u_t[ds(q, 1)]).then_inc(x_copied, 16)
                sc.dma_start(wu_dram[ds(q * (HALF // NT), HALF // NT)],
                             eu_s[ds(q * (HALF // NT), HALF // NT)]).then_inc(up_copied, 16)
                batch(0)
                batch(1)
                x_high(q + 1)
                batch(2)
                batch(3)

            x_high(0)
            first(0)
            first(1)
            with sc.Fori(2, NT) as q:
                first(q)
            for b in range(NB):
                g_evac((NT - 1) * NB + b, b, 0, NT - 1)
            weights_high(wd, wd_in, wd_h, 0, 1)
            weights_high(wu, wu_in, wu_h, 0, 1)
            for part in range(NT):
                steps = slice(HALF + part * (HALF // NT), HALF + (part + 1) * (HALF // NT))
                sc.dma_start(wu_dram[steps], eu_s[steps]).then_inc(up_rest, 16)

            def next_up_high(it, b):
                if not isinstance(it, int) or it > 0:
                    weights_high(wu, wu_in, wu_h, (b + 1) % 2, it * 2 - 2 + (b + 1) // 2 + 1)

            def next_down_high(it, b):
                weights_high(wd, wd_in, wd_h, (b + 1) % 2, it * 2 + (b + 1) // 2 + 1)

            def run_a(it, n, p, t):
                first = isinstance(it, int) and it == 0
                q = NT if first else reg(sc, n * NT + NT + t)
                q_par = 1 if first else 1 - p
                for b in range(NB):
                    if b == 0 and selects(n) and not first:
                        x_high(q)
                    if b or not first:
                        hid_high(it * PER + b - 1, (b - 1) % PER)
                    next_up_high(it, b)
                    next_down_high(it, b)
                    if b == 0 and selects(n):
                        x_place(q, q_par, t)
                    silu(it * PER + b, b)
                    g_evac(it * NB + NT * NB + b, b, 1, t)

            def run_b(it, n, p, t, attn):
                r = sc.snap((n - LAG) * NT + t) if attn else None
                for b in range(NB):
                    hid_high(it * PER + b - 1, (b - 1) % PER)
                    next_up_high(it, b)
                    if attn and b == 1:
                        sc.wait_ge(a_t, r + 1)
                        sc.copy(xaT[:].rearrange("p c n -> p (c n)"), ps_s[:]).then_inc(a_x, 1)
                    if attn and b == 2:
                        sc.wait_ge(a_z, r + 1)
                        sc.copy(zT[:], ps_s[0:RANK, 0:P]).then_inc(a_zc, 1)
                    next_down_high(it, b)
                    silu(it * PER + b, b)
                    if not is_last(n):
                        g_evac(it * NB + NT * NB + b, b, 0, t)
                    if attn and b == 3:
                        held(sc, "act", a_fin, r + 2)
                        sc.dma_start(x_in.rearrange("s t p d -> (s t) p d")[sc.snap((n - LAG + NBLK) * NT + t)],
                                     xaln[:]).then_inc(a_out, 16)

            run_a(0, 0, 0, 0)
            sc.dma_start(x_in[NSTAGE:NSTAGE + 1], u_t[0:1]).then_inc(block_out, 16)

            def run_last(it):
                hid_high(it * PER - 1, PER - 1)
                for b in range(PER - 1):
                    next_up_high(it, b)

            after = [False]

            def body(n, p, attn):
                iterations(sc, n, p, attn, run_a, run_b, run_last)
                if not attn and not after[0]:
                    sc.dma_start(x_in[ds(n * 2 + NT, 2)], u_t[ds(n * 2 + NT, 2)]).then_inc(x_rest, 16)
                after[0] = after[0] or attn
                held(sc, "act", evac_done, n * NT + NT)
                sc.dma_start(y_all[n].rearrange("t p d -> p t d"), yres[:]).then_inc(block_out, 16)

            stages(sc, body)
            sc.wait_ge(a_out, 16 + 16 * NT * NBLK)
            sc.wait_ge(x_copied, 16 * NT)

        @block.vector
        def _(dve):
            for t in range(TG):
                dve.memset(tq[NG * t:NG * t + NG, :], float(HK * t)).then_inc(tq_set, 1)
            dve.wait_ge(tq_set, TG)
            dve.wait_ge(consts, 1)
            dve.wait_ge(small_in, 16 * 7)
            for h in range(1, HEADS, 2):
                dve.wait_ge(k_tr, h + 2)
                dve.tensor_copy(wqT[:, h, :], ps_out[h][:]).then_inc(q_cp[1], 1)
            dve.wait_ge(a_pe, 1)
            dve.tensor_copy(stata[0:RANK, 0:12], ps_s[0:RANK, 0:12]).then_inc(fly, 1)
            dve.tensor_copy(stat[0:RANK, 0:12], ps_s[0:RANK, 12:24]).then_inc(fly, 1)
            c = 2

            def factor(lvl, i, j):
                at = lvl * 4 + i * 2 + j
                return stata[0:RANK, at:at + 1] if at < 12 else stat[0:RANK, at - 12:at - 11]

            for lvl in range(LEVELS):
                src = fw[:, 0 if lvl % 2 == 0 else 2, :].rearrange("r (a i b) -> r a i b", a=2 ** lvl, i=2)
                dst = fw[:, 2 if lvl % 2 == 0 else 0, :].rearrange("r (a i b) -> r a i b", a=2 ** lvl, i=2)
                dve.wait_ge(fly, c)
                for j in range(2):
                    dve.tensor_scalar(dst[:, :, j, :], src[:, :, 0, :], factor(lvl, 0, j), None, ALU.mult).then_inc(fly, 1)
                c += 2
                dve.wait_ge(fly, c)
                for j in range(2):
                    dve.scalar_tensor_tensor(out=dst[:, :, j, :], in0=src[:, :, 1, :], scalar=factor(lvl, 1, j),
                                             in1=dst[:, :, j, :], op0=ALU.mult, op1=ALU.add).then_inc(fly, 1)
                c += 2
            for i in range(2 * KC):
                dve.wait_ge(wk_h, i + 1)
                w = wk[:, :, i % KC, i // KC * 512:i // KC * 512 + 512]
                dve.tensor_tensor(w[:, L, :], ps_out[i % NT][:], w[:, H, :].bitcast(F32), ALU.subtract).then_inc(wk_l, 1)
            dve.wait_ge(a_pe, 2)
            dve.tensor_copy(Dv[:], ps_g[:].rearrange("p g q i -> p (g q i)")).then_inc(a_cp, 1)
            dve.wait_ge(a_pe, 3)
            dve.tensor_copy(fw[:, 3, :], ps_s[0:RANK, 0:RANK]).then_inc(a_cp, 1)
            dve.wait_ge(a_pe, 4)
            dve.tensor_copy(fw[:, 2, :], ps_s[0:RANK, 0:RANK]).then_inc(a_cp, 1)
            dve.wait_ge(a_pe, 5)
            dve.tensor_copy(M[:], ps_s[0:RANK, :]).then_inc(a_fin, 1)

            def down_weights_low(number, slot):
                held(dve, "dve", wd_h, number + 1)
                w = wd[:, slot, :]
                dve.tensor_tensor(w[:, D:2 * D], w[:, D:2 * D].bitcast(F32), w[:, 0:D].bitcast(F32), ALU.subtract).then_inc(wd_l, 1)

            def normalise(x, out, st, chain, base, done, number):
                dve.bn_stats(st[:, 0:6], x[:]).then_inc(chain, 1)
                held(dve, "dve", chain, base + 1)
                dve.bn_aggr(st[:, 6:8], st[:, 0:6]).then_inc(chain, 1)
                held(dve, "dve", chain, base + 2)
                dve.tensor_scalar(st[:, 7:8], st[:, 7:8], EPS, None, ALU.add).then_inc(chain, 1)
                held(dve, "dve", done, number + 1)
                dve.tensor_scalar(out[:], x[:], st[:, 6:7], st[:, 8:9], ALU.subtract, ALU.mult).then_inc(chain, 1)

            def sel_norm(q):
                held(dve, "dve", x_in_s, q * 16 + 16)
                normalise(xs, xs, stat, norm_c, q * NORM, rstd_done, q)

            def x_low(q):
                held(dve, "dve", s_xh, q + 1)
                dve.tensor_tensor(xt[:, L, :, :], ps_s[:].rearrange("p (c n) -> p c n", c=KC),
                                  xt[:, H, :, :].bitcast(F32), ALU.subtract).then_inc(s_xl, 1)

            sims = ps_s[:].rearrange("p (h s k) -> p h s k", h=2, s=2)

            def best(q, h2):
                held(dve, "dve", s_sim, q * 2 + h2 + 1)
                for h in range(2):
                    for s in range(2):
                        dve.max(v8[:, 2 * h2 + h, s, :], sims[:, h, s, :]).then_inc(sel_c, 1)
                held(dve, "dve", sel_c, q * SEL + 8 * h2 + 4)
                for h in range(2):
                    for s in range(2):
                        dve.max_index(i8[:, 2 * h2 + h, s, :], v8[:, 2 * h2 + h, s, :], sims[:, h, s, :]).then_inc(sel_c, 1)

            def merge_sums(q):
                def after(k):
                    held(dve, "dve", sel_c, q * SEL + k)

                after(16)
                dve.tensor_tensor(s64[:], v8[:, :, 0, :].unsqueeze(3).to_broadcast([P, HEADS, TOP, TOP]),
                                  v8[:, :, 1, :].unsqueeze(2).to_broadcast([P, HEADS, TOP, TOP]), ALU.add).then_inc(sel_c, 1)
                after(17)
                for h in range(HEADS):
                    ins = dve.max(f8[:, h, :], s64[:, h, :, :].rearrange("p a b -> p (a b)"))
                ins.then_inc(sel_c, 1)
                after(18)
                for h in range(HEADS):
                    ins = dve.max_index(pos[:, h * TOP:h * TOP + TOP], f8[:, h, :], s64[:, h, :, :].rearrange("p a b -> p (a b)"))
                ins.then_inc(sel_c, 1)

            def merge_experts(q):
                def after(k):
                    held(dve, "dve", sel_c, q * SEL + k)

                after(19)
                dve.tensor_scalar(j12[:, 0, :], pos[:], 3, None, ALU.logical_shift_right).then_inc(sel_c, 1)
                dve.tensor_scalar(j12[:, 1, :], pos[:], TOP - 1, None, ALU.bitwise_and).then_inc(sel_c, 1)
                after(21)
                dve.tensor_tensor(eq8, j12[:].unsqueeze(3).to_broadcast([P, 2, HK, TOP]),
                                  iota8[:].unsqueeze(1).unsqueeze(1).to_broadcast([P, 2, HK, TOP]),
                                  ALU.is_equal).then_inc(sel_c, 1)
                after(22)
                for s in range(2):
                    e = eq8[:, s, :, :].rearrange("p (h k) j -> p h k j", h=HEADS)
                    ins = dve.tensor_tensor(e, e, i8[:, :, s, :].unsqueeze(2).to_broadcast([P, HEADS, TOP, TOP]), ALU.mult)
                ins.then_inc(sel_c, 1)
                after(23)
                dve.tensor_reduce(i12[:], eq8, AX.X, ALU.add).then_inc(sel_c, 1)

            def merge_layout(q, par, t):
                def after(k):
                    held(dve, "dve", lay_c, q * LAY + k)

                held(dve, "dve", sel_c, q * SEL + SEL)
                dve.tensor_scalar(clamp[:], i12[:, 0, :], float(STEPS), float(P - 1), ALU.is_ge, ALU.mult)
                dve.tensor_scalar(raw[:, 0, :], i12[:, 0, :], float(STEPS - 1), tq[:, 0:1], ALU.min, ALU.add)
                dve.tensor_scalar(raw[:, 2, :], f8[:].rearrange("p h k -> p (h k)"), 0.0, None, ALU.max).then_inc(lay_c, 1)
                after(1)
                dve.tensor_tensor(raw[:, 1, :], i12[:, 1, :], clamp[:], ALU.max).then_inc(lay_c, 1)
                after(2)
                dve.transpose(raw_t, raw[:].rearrange("p a b -> p (a b)")).then_inc(lay_c, 1)
                after(3)
                dve.tensor_copy(part[:, 0, :], raw_t[:, 2 * NG:3 * NG])
                dve.tensor_copy(pick[:, par, t, 0:2, :], raw_t[:, 0:2 * NG].rearrange("p (a b) -> p a b", a=2)).then_inc(lay_c, 1)
                after(4)
                dve.tensor_tensor(rest[:, 0, :], raw_t[:, 2 * NG:3 * NG], part[:, 0, :], ALU.subtract)
                dve.tensor_copy(pick[:, par, t, 2, :], part[:, 0, :]).then_inc(lay_c, 1)
                after(5)
                dve.tensor_copy(part[:, 1, :], rest[:, 0, :]).then_inc(split_c, 1)
                held(dve, "dve", split_c, q * 2 + 1)
                dve.tensor_tensor(rest[:, 1, :], rest[:, 0, :], part[:, 1, :], ALU.subtract)
                dve.tensor_copy(pick[:, par, t, 3, :], part[:, 1, :]).then_inc(split_c, 1)
                held(dve, "dve", split_c, q * 2 + 2)
                dve.tensor_copy(pick[:, par, t, 4, :], rest[:, 1, :]).then_inc(picked, 1)

            raw_t = s64[:, 2:4, :, :].rearrange("p a b c -> p (a b c)")[:, 0:3 * NG]

            def one_hots(gb, b, half, par, t):
                held(dve, "dve", hot1_done, gb)
                held(dve, "dve", g_mm, gb - 1 if not isinstance(gb, int) else max(0, gb - 1))
                cols = TG * HALF
                dve.tensor_tensor(hot1_eq[:], iota1[:, half, :].unsqueeze(1).to_broadcast([P, GB, cols]),
                                  pick[:, par, t, 0, b * GB:b * GB + GB].unsqueeze(2).to_broadcast([P, GB, cols]),
                                  ALU.is_equal).then_inc(hot1_eqd, 1)
                dve.tensor_tensor(hot2[:, b % 2, :, :], iota2[:].unsqueeze(1).to_broadcast([P, GB, P]),
                                  pick[:, par, t, 1, b * GB:b * GB + GB].unsqueeze(2).to_broadcast([P, GB, P]),
                                  ALU.is_equal).then_inc(hot2_done, 1)

            def mult(S, j, i1):
                held(dve, "dve", silu_done, S + 1)
                dve.tensor_tensor(act[:, j % 2, :], act[:, j % 2, :], G[:, i1, :], ALU.mult).then_inc(mult_done, 1)

            def first(q):
                batch = lambda b: None if isinstance(q, int) and q == 0 else one_hots((q - 1) * NB + b, b, 0, 0, q - 1)
                if not isinstance(q, int) or q > 0:
                    merge_experts(q - 1)
                best(q, 0)
                if not isinstance(q, int) or q > 0:
                    merge_layout(q - 1, 0, q - 1)
                batch(0)
                best(q, 1)
                batch(1)
                sel_norm(q + 1)
                batch(2)
                x_low(q + 1)
                batch(3)
                merge_sums(q)

            sel_norm(0)
            x_low(0)
            first(0)
            first(1)
            with dve.Fori(2, NT) as q:
                first(q)
            merge_experts(NT - 1)
            merge_layout(NT - 1, 0, NT - 1)
            for b in range(NB):
                one_hots((NT - 1) * NB + b, b, 0, 0, NT - 1)
            one_hots(NT * NB, 0, 1, 0, 0)
            down_weights_low(0, 0)

            def run_a(it, n, p, t, nxt):
                first = isinstance(it, int) and it == 0
                q = NT if first else reg(dve, n * NT + NT + t)
                q_par = 1 if first else 1 - p
                tile0 = isinstance(t, int) and t == 0
                tile3 = isinstance(t, int) and t == NT - 1
                i1 = 0 if tile0 else t * PER
                gb = it * NB + NT * NB
                sel = selects(n)
                if sel and not first:
                    x_low(q)
                one_hots(gb + 1, 1, 1, p, t)
                down_weights_low(it * PER + 1, 1)
                if sel and not tile0:
                    merge_experts(q - 1)
                held(dve, "dve", g_out, gb)
                mult(it * PER, 0, i1)
                if sel:
                    best(q, 0)

                one_hots(gb + 2, 2, 1, p, t)
                down_weights_low(it * PER + 2, 0)
                mult(it * PER + 1, 1, i1 + 1)
                if sel:
                    sel_norm(q + 1)

                one_hots(gb + 3, 3, 1, p, t)
                down_weights_low(it * PER + 3, 1)
                if sel and not tile0:
                    merge_layout(q - 1, q_par, t - 1)
                if sel:
                    best(q, 1)
                mult(it * PER + 2, 2, i1 + 2)

                if sel:
                    merge_sums(q)
                if tile0 and not first:
                    evacuate(n - 1)
                down_weights_low(it * PER + 4, 0)
                if tile0:
                    mult(it * PER + 3, 3, i1 + 3)
                if nxt:
                    one_hots(gb + 4, 0, 0 if tile3 else 1, *nxt)
                if not tile0:
                    mult(it * PER + 3, 3, i1 + 3)

            def run_b(it, n, p, t, attn, nxt):
                r = dve.snap((n - LAG) * NT + t) if attn else None
                tile0 = isinstance(t, int) and t == 0
                tile3 = isinstance(t, int) and t == NT - 1
                gb = it * NB + NT * NB
                for b in range(NB):
                    if is_last(n):
                        pass
                    elif b + 1 < NB:
                        one_hots(gb + b + 1, b + 1, 0, 1 - p, t)
                    else:
                        one_hots(gb + b + 1, 0, 1 if tile3 else 0, *nxt)
                    down_weights_low(it * PER + b + 1, (b + 1) % 2)
                    if attn and b == 0:
                        held(dve, "dve", xa_in, r * 16 + 16)
                        held(dve, "dve", a_out, r * 16 + 16)
                        normalise(xa, xaln, stata, att_c, r * ATT, arstd_done, r)
                    if b == 0:
                        held(dve, "dve", g_out, (n * ITERS + NT) * NB + NT * NB if is_last(n) else gb)
                    mult(it * PER + b, b, t * PER + (HALF + b))
                    if b == 1 and tile0 and not is_last(n):
                        merge_experts(n * NT + NT + NT - 1)
                        merge_layout(n * NT + NT + NT - 1, 1 - p, NT - 1)
                    if attn and b == 2:
                        held(dve, "dve", a_du, r * 2 + 2)
                        held(dve, "dve", a_y, r + 1)
                        dve.tensor_tensor(xaln[:], ps_s[:], xaln[:], ALU.add).then_inc(a_fin, 1)

            def run_last(it):
                evacuate(NSTAGE - 1)

            def evacuate(n):
                held(dve, "dve", up_done, n * STEPS + STEPS)
                held(dve, "dve", res_in, n * 16 + 16)
                for tile in range(NT):
                    dve.scalar_tensor_tensor(out=yres[:, tile, :], in0=ps_out[tile][:], scalar=0.5, in1=yres[:, tile, :],
                                             op0=ALU.mult, op1=ALU.add).then_inc(evac_done, 1)

            run_a(0, 0, 0, 0, (0, 1))
            stages(dve, lambda n, p, attn: iterations_ahead(dve, n, p, attn, run_a, run_b, run_last))

        @block.tensor
        def _(pe):
            def three(out, lhs, rhs, first, last, **kw):
                ins = None
                for k, (a, b) in enumerate(((H, H), (H, L), (L, H))):
                    ins = pe.matmul(out, lhs(a), rhs(b), start=first and k == 0, stop=last and k == 2, **kw)
                return ins

            pe.wait_ge(consts, 1)
            pe.wait_ge(small_in, 16 * 7)
            for h in range(HEADS):
                ins = pe.transpose(ps_s[:, h * P:h * P + P], keys_raw[:, h * P:h * P + P], ident[:])
            ins.then_inc(k_tr, 1)
            for h in range(HEADS):
                for c in range(KC):
                    ins = pe.transpose(ps_out[h][:, c * P:c * P + P], wq_raw[:, c, h * P:h * P + P], ident[:])
                ins.then_inc(k_tr, 1)
            pe.wait_ge(k_set, 2)
            pe.wait_ge(q_cp[0], HEADS // 2)
            pe.wait_ge(q_cp[1], HEADS // 2)
            pe.matmul(ps_s[0:RANK, 0:LEVELS * 4], ones[:, 0:RANK], xa[0:1, 0:LEVELS * 4], start=True, stop=True).then_inc(a_pe, 1)
            pe.wait_ge(a_out, 16)
            pe.matmul(ps_g[:].rearrange("p g q i -> p (g q i)"), ones, G[0:1, KC + 1, :], start=True, stop=True).then_inc(a_pe, 1)
            for i in range(2 * KC):
                if i >= NT:
                    pe.wait_ge(wk_l, i - NT + 1)
                for h in range(2):
                    head = i // KC * 2 + h
                    ins = pe.matmul(ps_out[i % NT][:, h * 2 * NK:(h + 1) * 2 * NK],
                                    wqT[:, head, i % KC * P:i % KC * P + P], keysT[:, head, :], start=True, stop=True)
                ins.then_inc(wk_mm, 1)
            pe.wait_ge(fly, 2 + 4 * LEVELS)
            at = 0 if LEVELS % 2 == 0 else 2
            pe.transpose(ps_s[0:RANK, 0:RANK], fw[:, at, :], ident[0:RANK, 0:RANK]).then_inc(a_pe, 1)
            pe.wait_ge(a_cp, 2)
            pe.matmul(ps_s[0:RANK, 0:RANK], fw[:, 1, :], fw[:, 3, :], start=True, stop=True).then_inc(a_pe, 1)
            pe.wait_ge(a_cp, 3)
            pe.matmul(ps_s[0:RANK, :], fw[:, 2, :], xaln[0:RANK, :], start=True, stop=True).then_inc(a_pe, 1)

            def w_transpose(i, k):
                held(pe, "pe", raw_in[k], i * 16 + 16)
                for j in range(PER):
                    held(pe, "pe", w_cp, max(0, (i * 2 + k) * PER + j - 1) if isinstance(i, int) else (i * 2 + k) * PER + (j - 1))
                    for c in range(KC):
                        ins = pe.transpose(ps_hd[j % 2][:, c * P:c * P + P], G[:, RAW0 + k * PER + j, c * P:c * P + P], ident[:])
                    ins.then_inc(w_tr, 1)

            def transposes(q, atts):
                held(pe, "pe", norm_c, q * NORM + 4)
                if not isinstance(q, int) or q > 0:
                    held(pe, "pe", sel_c, q * SEL + (SEL_IDX1 - SEL))
                if atts is not None:
                    held(pe, "pe", a_fin, atts + 1)
                for c in range(KC):
                    ins = pe.transpose(ps_s[:, c * P:c * P + P], xs[:, c * P:c * P + P], ident[:])
                ins.then_inc(s_t, 1)

            def scores(q, h2):
                if h2 == 0:
                    held(pe, "pe", s_xl, q + 1)
                else:
                    held(pe, "pe", sel_c, q * SEL + SEL_IDX0)
                for c in range(KC):
                    ins = three(ps_s[:], lambda a: xt[:, a, c, :], lambda b: wk[:, b, c, h2 * 512:h2 * 512 + 512],
                                c == 0, c == KC - 1)
                ins.then_inc(s_sim, 1)

            def g_batch(gb, b):
                held(pe, "pe", hot2_done, gb + 1)
                held(pe, "pe", hot1_done, gb + 1)
                held(pe, "pe", g_out, gb)
                for g in range(GB):
                    for k in range(3):
                        ins = pe.matmul(ps_g[:, g, :, :].rearrange("p q i -> p (q i)"), hot2[:, b % 2, g, :], hot1[:, b % 2, k, g, :],
                                        start=k == 0, stop=k == 2)
                ins.then_inc(g_mm, 1)

            def down(it, j, par):
                S = it * PER + j
                held(pe, "pe", wd_l, S + 1)
                held(pe, "pe", silu_done, S - 1 if not isinstance(S, int) else max(0, S - 1))
                for c in range(KC):
                    ins = three(ps_hd[j % 2][:], lambda a: wd[:, j % 2, a * D + c * P:a * D + c * P + P],
                                lambda b: xT[:, par, b, c, :], c == 0, c == KC - 1)
                ins.then_inc(down_done, 1)

            def up(it, j):
                held(pe, "pe", wu_l, it * PER - PER + j + 1)
                held(pe, "pe", hidl_done, it * PER - PER + j + 1)
                for t in range(NT):
                    ins = three(ps_out[t][:], lambda a: hid[:, j, a, t * P:t * P + P],
                                lambda b: wu[:, j % 2, b * D:b * D + D], False, False, skip_group_check=True)
                ins.then_inc(up_done, 1)

            def clear_out():
                for t in range(NT):
                    pe.matmul(ps_out[t][:].rearrange("p (a b) -> p a b", b=P), zer[:], zer[:].unsqueeze(1).to_broadcast([P, NT, P]), start=True, stop=True, skip_group_check=True)

            pe.wait_ge(a_fin, 1)
            def first(q):
                batch = lambda b: None if isinstance(q, int) and q == 0 else g_batch((q - 1) * NB + b, b)
                w_transpose(q, 0)
                w_transpose(q, 1)
                scores(q, 1)
                batch(0)
                batch(1)
                transposes(q + 1, None)
                batch(2)
                scores(q + 1, 0)
                batch(3)

            transposes(0, 0)
            scores(0, 0)
            first(0)
            first(1)
            with pe.Fori(2, NT) as q:
                first(q)
            for b in range(NB):
                g_batch((NT - 1) * NB + b, b)
            clear_out()

            def run_a(it, n, p, t, atts):
                first = isinstance(it, int) and it == 0
                q = NT if first else reg(pe, n * NT + NT + t)
                q_par = 1 if first else 1 - p
                sel = selects(n)
                if isinstance(t, int):
                    held(pe, "pe", s_xt, q)
                for b in range(NB):
                    if b == 0 and sel and not first:
                        transposes(q, atts)
                    if not first:
                        up(it, b)
                    if b == 0 and sel and not first:
                        scores(q, 0)
                    if b == 2 and sel:
                        scores(q, 1)
                    down(it, b, p)
                    g_batch(it * NB + NT * NB + b, b)

            def run_b(it, n, p, t, attn):
                r = pe.snap((n - LAG) * NT + t) if attn else None
                for b in range(NB):
                    up(it, b)
                    if attn and b == 1:
                        held(pe, "pe", att_c, r * ATT + 4)
                        held(pe, "pe", sel_c, n * (NT * SEL) + ((2 * NT - 1) * SEL + SEL_IDX1))
                        held(pe, "pe", a_fin, r + 1)
                        for c in range(KC):
                            ins = pe.transpose(ps_s[:, c * P:c * P + P], xaln[:, c * P:c * P + P], ident[:])
                        ins.then_inc(a_t, 1)
                    if attn and b == 2:
                        held(pe, "pe", a_zc, r + 1)
                        pe.matmul(ps_s[:], zT[:], M[:], start=True, stop=True).then_inc(a_y, 1)
                    down(it, b, p)
                    if not is_last(n):
                        g_batch(it * NB + NT * NB + b, b)
                    if attn and b == 1:
                        held(pe, "pe", a_x, r + 1)
                        for c in range(KC):
                            ins = pe.matmul(ps_s[0:RANK, 0:P], wb[:, c, :], xaT[:, c, :], start=c == 0, stop=c == KC - 1)
                        ins.then_inc(a_z, 1)

            run_a(0, 0, 0, 0, 0)

            def body(n, p, attn):
                before = (n - LAG) * NT if attn else None
                with pe.Fori(1, NT) as t:
                    run_a(pe.snap(n * ITERS + t), n, p, t, None)
                with pe.Fori(0, NT) as t:
                    run_b(pe.snap(n * ITERS + NT + t), n, p, t, attn)
                if is_last(n):
                    for b in range(PER):
                        up(n * ITERS + ITERS, b)
                    return
                run_a(reg(pe, n * ITERS + ITERS), n + 1, 1 - p, 0, before + NT if attn else atts_done[0])
                held(pe, "pe", evac_done, n * NT + NT)
                clear_out()

            atts_done = [0]

            def body_counted(n, p, attn):
                body(n, p, attn)
                if attn:
                    atts_done[0] = NT * NBLK

            stages(pe, body_counted)


_INS = {"u": "L0_attn_u", "A_factors": "L0_attn_A_factors", "W_b_rank": "L0_attn_W_b_rank", "W_b_state": "L0_attn_W_b_state",
        "W_c_rank": "L0_attn_W_c_rank", "W_c_model": "L0_attn_W_c_model", "D_vec": "L0_attn_D_vec", "Wq": "L0_ffn_Wq",
        "keys": "L0_ffn_keys", "e_down": "L0_ffn_e_down", "e_up": "L0_ffn_e_up"}


def kernel(**inputs):
    import numpy as _np
    import concourse.bacc as _bacc
    from concourse import mybir as _mybir
    from concourse.bass_utils import run_bass_kernel_spmd as _run

    nc = _bacc.Bacc("TRN2", target_bir_lowering=False, num_devices=1)
    arrays, args = {}, []
    for short, name in _INS.items():
        a = _np.ascontiguousarray(inputs[name])
        arrays[f"in_{short}"] = a
        args.append(nc.dram_tensor(f"in_{short}", a.shape, _mybir.dt.from_np(a.dtype), kind="ExternalInput").ap())
    shape = inputs["L0_attn_u"].shape
    blocks = shape[0] * shape[1] // 512
    y = nc.dram_tensor("y_all", (2 * blocks, 4, 128, shape[2]), _mybir.dt.float32, kind="ExternalOutput").ap()
    macaron(nc, *args, y)
    r = _run(nc, [arrays], core_ids=[0])
    return r.results[0]["y_all"][blocks:].reshape(shape)
```
